# Optimizing a Trainium2 kernel written in Bass

```python
import numpy as np
import jax
import jax.numpy as jnp

def _softmax(x, axis=-1):
    return jax.nn.softmax(x, axis=axis)

def _gelu(x):
    return jax.nn.gelu(x, approximate=True)

def _silu(x):
    return jax.nn.silu(x)

def _sigmoid(x):
    return jax.nn.sigmoid(x)

def _layernorm(x, axis=-1, eps=1e-05):
    m = jnp.mean(x, axis=axis, keepdims=True)
    v = jnp.var(x, axis=axis, keepdims=True)
    return (x - m) / jnp.sqrt(v + eps)

def _scatter_add(tgt, idx, src, axis=0):
    return tgt.at[idx].add(src)

def _segment_sum(src, seg, n):
    return jax.ops.segment_sum(src, seg, n)
kernel_name = 'mk_adaln_d1_jaxref_r8_d33931'

def setup_inputs(seed: int=0):
    np.random.seed(seed)
    _w = jnp.asarray

    def _L0_attn_setup():
        import jax, jax.numpy as jnp
        import numpy as np
        B, S, HID = (1, 512, 256)
        NH, NKV, D = (16, 4, 128)
        QPG = NH // NKV
        GROUP = (QPG + 2) * D
        TOTAL = NKV * GROUP
        key = jax.random.key(seed)
        k0, k1, k2 = jax.random.split(key, 3)
        x = jax.random.normal(k0, (B, S, HID), dtype=jnp.float32)
        weight_qkv = jax.random.normal(k1, (TOTAL, HID), dtype=jnp.float32) * 0.02
        weight_proj = jax.random.normal(k2, (HID, NH * D), dtype=jnp.float32) * 0.02
        return {'x': x, 'weight_qkv': weight_qkv, 'weight_proj': weight_proj}
    _L0_attn_in = _L0_attn_setup()

    def _L0_ffn_setup():
        import jax, jax.numpy as jnp
        import numpy as np
        HIDDEN = 256
        INTER = 1024
        SCALE = 64.0

        def fwht(x):
            orig_shape = x.shape
            n = orig_shape[-1]
            x = x.reshape(-1, n)
            h = 1
            while h < n:
                x = x.reshape(-1, n // (2 * h), 2, h)
                a, b = (x[:, :, 0, :], x[:, :, 1, :])
                x = jnp.stack([a + b, a - b], axis=2).reshape(-1, n)
                h *= 2
            return (x / jnp.sqrt(jnp.asarray(n, x.dtype))).reshape(orig_shape)
        key = jax.random.key(seed)
        ks = jax.random.split(key, 8)
        inp = jax.random.normal(ks[0], (4, 256, HIDDEN), dtype=jnp.float32)
        SU_ug = jnp.where(jax.random.bernoulli(ks[1], 0.5, (HIDDEN,)), 1.0, -1.0).astype(jnp.float32)
        SU_dp = jnp.where(jax.random.bernoulli(ks[2], 0.5, (INTER,)), 1.0, -1.0).astype(jnp.float32)
        Wscale_ug = jax.random.uniform(ks[3], (2 * INTER,), jnp.float32, 0.5, 1.5)
        Wscale_dp = jax.random.uniform(ks[4], (HIDDEN,), jnp.float32, 0.5, 1.5)
        W_up = jax.random.normal(ks[5], (INTER, HIDDEN), dtype=jnp.float32) * 0.02
        W_gate = jax.random.normal(ks[6], (INTER, HIDDEN), dtype=jnp.float32) * 0.02
        W_down = jax.random.normal(ks[7], (HIDDEN, INTER), dtype=jnp.float32) * 0.02
        return {'input': inp, 'SU_ug': SU_ug, 'SU_dp': SU_dp, 'Wscale_ug': Wscale_ug, 'Wscale_dp': Wscale_dp, 'W_up': W_up, 'W_gate': W_gate, 'W_down': W_down}
    _L0_ffn_in = _L0_ffn_setup()
    _L0_c = _w((lambda *s: np.random.randn(*s).astype(np.float32) * 0.05)(2, 256))
    _L0_wmod = _w((lambda *s: np.random.randn(*s).astype(np.float32) * 0.05)(256, 6 * 256) * 256 ** (-0.5))
    _d = {'L0_attn_x': _L0_attn_in['x'], 'L0_attn_weight_qkv': _L0_attn_in['weight_qkv'], 'L0_attn_weight_proj': _L0_attn_in['weight_proj'], 'L0_ffn_SU_ug': _L0_ffn_in['SU_ug'], 'L0_ffn_SU_dp': _L0_ffn_in['SU_dp'], 'L0_ffn_Wscale_ug': _L0_ffn_in['Wscale_ug'], 'L0_ffn_Wscale_dp': _L0_ffn_in['Wscale_dp'], 'L0_ffn_W_up': _L0_ffn_in['W_up'], 'L0_ffn_W_gate': _L0_ffn_in['W_gate'], 'L0_ffn_W_down': _L0_ffn_in['W_down'], 'L0_c': _L0_c, 'L0_wmod': _L0_wmod}
    _x0 = _d['L0_attn_x']
    _d['L0_attn_x'] = jax.random.normal(jax.random.fold_in(jax.random.key(seed), 1), (2, 1024, 256), dtype=_x0.dtype)
    del _x0
    return _d

def reference(L0_attn_x, L0_attn_weight_qkv, L0_attn_weight_proj, L0_ffn_SU_ug, L0_ffn_SU_dp, L0_ffn_Wscale_ug, L0_ffn_Wscale_dp, L0_ffn_W_up, L0_ffn_W_gate, L0_ffn_W_down, L0_c, L0_wmod):

    def _L0_attn_ref(x, weight_qkv, weight_proj):
        import jax, jax.numpy as jnp
        import numpy as np
        B, S, HID = (1, 512, 256)
        NH, NKV, D = (16, 4, 128)
        QPG = NH // NKV
        GROUP = (QPG + 2) * D
        TOTAL = NKV * GROUP
        b, s, _ = x.shape
        qkv = jnp.einsum('bsh,ph->bsp', x, weight_qkv).reshape(b, s, NKV, GROUP)
        q = qkv[..., :QPG * D].reshape(b, s, NKV, QPG, D)
        k = qkv[..., QPG * D:(QPG + 1) * D]
        v = qkv[..., (QPG + 1) * D:]
        scale = 1.0 / jnp.sqrt(jnp.float32(D))
        scores = jnp.einsum('bsgqd,btgd->bgqst', q, k) * scale
        causal = jnp.tril(jnp.ones((s, s), dtype=bool))
        scores = jnp.where(causal, scores, jnp.finfo(scores.dtype).min)
        attn = jax.nn.softmax(scores, axis=-1)
        out = jnp.einsum('bgqst,btgd->bsgqd', attn, v)
        out = out.reshape(b, s, NH * D)
        return jnp.einsum('bse,he->bsh', out, weight_proj)

    def _L0_ffn_ref(input, SU_ug, SU_dp, Wscale_ug, Wscale_dp, W_up, W_gate, W_down):
        import jax, jax.numpy as jnp
        import numpy as np
        HIDDEN = 256
        INTER = 1024
        SCALE = 64.0

        def fwht(x):
            orig_shape = x.shape
            n = orig_shape[-1]
            x = x.reshape(-1, n)
            h = 1
            while h < n:
                x = x.reshape(-1, n // (2 * h), 2, h)
                a, b = (x[:, :, 0, :], x[:, :, 1, :])
                x = jnp.stack([a + b, a - b], axis=2).reshape(-1, n)
                h *= 2
            return (x / jnp.sqrt(jnp.asarray(n, x.dtype))).reshape(orig_shape)
        n = SU_ug.shape[0]
        x = input.reshape(-1, n)
        x = fwht(x * SU_ug) / SCALE
        x_up = x @ W_up.T * (Wscale_ug[:INTER] * SCALE)
        x_gate = x @ W_gate.T * (Wscale_ug[INTER:] * SCALE)
        x = jax.nn.silu(x_gate) * x_up
        x = fwht(x * SU_dp) / SCALE
        x = x @ W_down.T * (Wscale_dp * SCALE)
        return x.reshape(input.shape)
    x = L0_attn_x
    mod = (_silu(L0_c) @ L0_wmod).reshape(L0_c.shape[0], 6, 1, -1)
    sa, ca, ga, sb, cb, gb = (mod[:, 0], mod[:, 1], mod[:, 2], mod[:, 3], mod[:, 4], mod[:, 5])
    ga = (2 * (ga >= 0) - 1) * jnp.maximum(jnp.abs(ga), 0.25)
    gb = (2 * (gb >= 0) - 1) * jnp.maximum(jnp.abs(gb), 0.25)
    h = _layernorm(x, axis=-1) * (1 + ca) + sa
    x = x + ga * _L0_attn_ref(h, L0_attn_weight_qkv, L0_attn_weight_proj)
    h = _layernorm(x, axis=-1) * (1 + cb) + sb
    x = x + gb * _L0_ffn_ref(h, L0_ffn_SU_ug, L0_ffn_SU_dp, L0_ffn_Wscale_ug, L0_ffn_Wscale_dp, L0_ffn_W_up, L0_ffn_W_gate, L0_ffn_W_down)
    return x

_drawn_inputs = setup_inputs


def setup_inputs(seed=0):
    import zlib

    import numpy as np

    out = dict(_drawn_inputs(seed))
    spreads = {}
    factors = {}
    for name, (base, spread) in spreads.items():
        noise = np.random.default_rng([zlib.crc32(name.encode()), seed]).standard_normal(out[name].shape)
        drawn = base * np.exp(spread * noise) if base else spread * noise
        out[name] = jnp.asarray(drawn.astype(out[name].dtype))
    for name, factor in factors.items():
        out[name] = (out[name] * factor).astype(out[name].dtype)
    return out
```

```python
import numpy as np
import concourse.bass as bass
from concourse import mybir
from contextlib import ExitStack

F32 = mybir.dt.float32
F32R = mybir.dt.float32r
BF16 = mybir.dt.bfloat16
ALU = mybir.AluOpType
ACT = mybir.ActivationFunctionType
AX = mybir.AxisListType

P = 128
B, SEQ, HID = 2, 1024, 256
NKV, QPG, D = 4, 4, 128
INTER = 1024
KH = HID // P
NT = SEQ // P
NM = INTER // P
CH = 512
CT = CH // P
NC_B = SEQ // CH
GW = (QPG + 2) * D
SCALE = float(D) ** -0.5
EPS = 1e-5
MASKED = -1e30
STEPS = [NT - 1 - s for s in range(NT)]
UNITS = [(i, j) for i in STEPS for j in range(i + 1)]
NU = len(UNITS)
LAST = {i: max(n for n, u in enumerate(UNITS) if u[0] == i) for i in STEPS}
SA, CA, GA, SB, CB, GB = range(6)


def walk():
    out = [("S", STEPS[0], h) for h in range(QPG)]
    lag, done = 2, 0

    def values(n):
        out.append(("V", n, 0))
        i, j = UNITS[n]
        if i < STEPS[0] and j == min(1, i):
            out.append(("Y", i + 1, 0))

    for n, (i, j) in enumerate(UNITS):
        for h in range(QPG):
            if i and j == h * (i + 1) // (QPG + 1):
                out.append(("S", i - 1, h))
        out.append(("T", n, 0))
        if n >= lag:
            values(n - lag)
    for n in range(NU - lag, NU):
        values(n)
    out.append(("Y", 0, 0))
    return out


WALK = walk()


def halves(i):
    n = (i + 1) * P
    return (2, n // 2) if n > CH else (1, n)


def build(nc, x_in, wqkv, wproj, wmod, c_cols, wug, wdn, su_ug, su_dp, ws_ug, ws_dp, ident_in, mask_in, had_in, out):
    ctx = ExitStack()
    with ctx:
        def sb(name, shape, dt=F32):
            return ctx.enter_context(nc.sbuf_tensor(name, shape, dt))

        def sem(name):
            return ctx.enter_context(nc.semaphore(name))

        x = sb("x", [P, B * NT, HID])
        h_hi = sb("h_hi", [P, KH, B * SEQ], F32R)
        h_lo = sb("h_lo", [P, KH, B * SEQ], F32R)
        q_hi = sb("q_hi", [P, QPG, SEQ], F32R)
        q_lo = sb("q_lo", [P, QPG, SEQ], F32R)
        k_hi = sb("k_hi", [P, SEQ], F32R)
        k_lo = sb("k_lo", [P, SEQ], F32R)
        v_hi = sb("v_hi", [P, NT, D], F32R)
        v_lo = sb("v_lo", [P, NT, D], F32R)
        vt = sb("vt", [P, SEQ])
        prob = sb("prob", [P, 2, QPG, SEQ])
        pt_hi = sb("pt_hi", [P, 3, CH], F32R)
        pt_lo = sb("pt_lo", [P, 3, CH], F32R)
        o_hi = sb("o_hi", [P, 2, CH], F32R)
        o_lo = sb("o_lo", [P, 2, CH], F32R)
        w_raw = sb("w_raw", [P, KH, GW])
        w_hi = sb("w_hi", [P, KH, GW], F32R)
        w_lo = sb("w_lo", [P, KH, GW], F32R)
        wp_raw = sb("wp_raw", [P, QPG, HID])
        wp_hi = sb("wp_hi", [P, QPG, HID], F32R)
        wp_lo = sb("wp_lo", [P, QPG, HID], F32R)
        ga_row = sb("ga_row", [P, B, HID])
        cols = sb("cols", [P, 6, KH, B])
        ident = sb("ident", [P, P])
        ident_b = sb("ident_b", [P, P], BF16)
        mask_b = sb("mask_b", [P, P], BF16)
        nmax = sb("nmax", [P, 2, QPG])
        rsum = sb("rsum", [P, 2, QPG])
        rinv = sb("rinv", [P, 2, QPG])
        stats = sb("stats", [P, CT, 6])
        mv = sb("mv", [P, CT, 2])
        vare = sb("vare", [P, CT])
        rstd = sb("rstd", [P, CT])
        mhalf = sb("mhalf", [P, CT])
        su_u = sb("su_u", [P, KH])
        su_d = sb("su_d", [P, NM])
        ws_u = sb("ws_u", [P, 2 * NM])
        ws_d = sb("ws_d", [P, KH])
        sc = sb("sc", [P, 4, KH, B])
        scb = sb("scb", [P, KH, B, P])

        flat = prob[:, :, :, :].rearrange("p a h n -> p (a h n)")

        def part(start, *shape):
            size = int(np.prod(shape))
            names = "abcd"[:len(shape)]
            return flat[:, start:start + size].rearrange(
                f"p ({' '.join(names)}) -> p {' '.join(names)}", **dict(zip(names, shape)))

        xhat = part(0, CT, HID)
        h32 = part(1024, KH, CH)
        wmod_sb = part(2048, KH, 6 * HID)
        mask_f = part(5120, 1, P)
        had_sb = part(2048, 2, P)
        raw = part(2304, KH, CH)
        fly = part(3328, KH, CH)
        raw_d = part(4352, NM, HID)
        g32 = part(0, 2, CH)
        silu = part(1024, 2, CH)
        yt = part(2048, KH, CH)
        o_out = part(3072, CT, HID)
        raw_d2 = part(2304, NM, HID)
        guard_a, guard_b = part(5248, B, HID), part(5760, B, HID)
        had_r = w_hi[:, 0, CH:CH + 2 * P].rearrange("p (a n) -> p a n", a=2)
        fly_hi = w_hi[:, :, 0:CH]
        fly_lo = w_lo[:, :, 0:CH]
        h2_hi = q_hi[:, :, :].rearrange("p (k b) n -> p k (b n)", k=KH)
        h2_lo = q_lo[:, :, :].rearrange("p (k b) n -> p k (b n)", k=KH)
        wu_hi, wu_lo = h_hi, h_lo
        wd_hi = [a[:, :].rearrange("p (m n) -> p m n", m=4) for a in (k_hi, k_lo)]
        wd_lo = [a[:, :, :].rearrange("p m d -> p (m d)").rearrange("p (m n) -> p m n", m=4) for a in (v_hi, v_lo)]
        g_hi, g_lo = pt_hi, pt_lo

        psum = [ctx.enter_context(nc.psum_tensor(f"ps{n}", [P, 2 * CH], F32)) for n in range(4)]
        S = [psum[0], psum[1]]
        T = [psum[2][:, 0:CH], psum[2][:, CH:2 * CH]]
        O = psum[3][:, 0:CH]
        Y = psum[3][:, CH:2 * CH]

        x_in_s = sem("x_loaded")
        small_s = sem("small_loaded")
        wmod_s = sem("wmod_loaded")
        wraw_s = sem("w_raw_loaded")
        wpraw_s = sem("wp_raw_loaded")
        consts = sem("constants_made")
        silu_e = sem("mod_exp")
        silu_c = sem("mod_silu")
        mod_mm = sem("mod_multiplied")
        mod_ok = sem("mod_ready")
        dve_self = sem("dve_self")
        pool_self = sem("pool_self")
        dve_gate, pool_gate = sem("dve_gate"), sem("pool_gate")
        ln = [{k: sem(f"ln{r}_{k}") for k in
               ("stats", "aggr", "vare", "rstd", "xhat", "tr", "mod", "hi", "lo")} for r in range(2)]
        qkv_done, qkv_hi, qkv_lo = sem("qkv_done"), sem("qkv_hi"), sem("qkv_lo")
        vt_done, vtr_done, v_hi_s, v_lo_s = sem("vt_done"), sem("vtr_done"), sem("v_hi_done"), sem("v_lo_done")
        s_done, max_done, exp_done = sem("scores_done"), sem("max_done"), sem("exp_done")
        rinv_done, prob_done = sem("rinv_done"), sem("prob_done")
        t_done, pth_done, ptl_done = sem("transposed"), sem("pt_hi_done"), sem("pt_lo_done")
        pv_done, oh_done, ol_done = sem("pv_done"), sem("o_hi_done"), sem("o_lo_done")
        y_done, add_done = sem("y_done"), sem("x_added")
        w_ready, wp_ready = sem("w_ready"), sem("wp_ready")
        raw_s = [sem(f"raw_loaded{n}") for n in range(2)]
        rawd_s, had_s, had_ok = sem("raw_d_loaded"), sem("had_loaded"), sem("had_ready")
        fly_s, flyhi_s, fly_ok, fmm_s, fhi_s, wf_ok = (sem("fly"), sem("fly_hi"), sem("fly_ready"),
                                                       sem("hadamard_done"), sem("wf_hi"), sem("wf_ready"))
        gu_s, silu_s, g32_s, ghi_s, g_ok = sem("gate_up_done"), sem("silu_done"), sem("g32_done"), sem("g_hi_done"), sem("g_ready")
        dn_s, yt_s, ytr_s, fin_s, out_s = sem("down_done"), sem("yt_done"), sem("y_transposed"), sem("out_ready"), sem("out_stored")

        PER_PE = {qkv_done: 12, vtr_done: 2, s_done: 32, t_done: NU, pv_done: NU, y_done: NT}
        PER_ACT = {qkv_hi: 10, vt_done: 2, v_hi_s: 2, exp_done: 32, pth_done: NU, oh_done: NT}
        PER_DVE = {qkv_lo: 10, v_lo_s: 2, max_done: 32, rinv_done: 32, ptl_done: NU, ol_done: NT, add_done: NT}
        PER_POOL = {prob_done: 32}
        per = {s.name: n for d in (PER_PE, PER_ACT, PER_DVE, PER_POOL) for s, n in d.items()}
        TURNS = B * NKV

        def this(s, t, k):
            return (t + 1) * per[s.name] + k

        CHUNKS = [("v", 0, 0), ("v", 0, 1), ("k", 0, 0), ("k", 0, 1)]
        CHUNKS += [("q", h, 1) for h in range(QPG)] + [("q", h, 0) for h in range(QPG)]
        V_AFTER = 5

        def bank(c):
            return psum[c % 4 // 2][:, c % 2 * CH:(c % 2 + 1) * CH]

        block = ctx.enter_context(nc.Block())

        @block.sync
        def _(sp):
            sp.sem_inc(out_s, 16)
            for c in range(B * NC_B):
                sp.dma_start(x[:, c * CT:(c + 1) * CT, :],
                             x_in[c * CT:(c + 1) * CT, :, :].rearrange("t p n -> p t n")).then_inc(x_in_s, 16)
            sp.dma_start(w_raw[:, :, :], wqkv[0, :, :].rearrange("p (k n) -> p k n", k=KH)).then_inc(wraw_s, 16)
            with sp.Fori(0, B) as b:
                with sp.Fori(0, NKV) as g:
                    t = b * NKV + g
                    sp.wait_ge(wp_ready, t + 1)
                    sp.dma_start(wp_raw[:, :, :],
                                 wproj[bass.ds(g, 1), :, :].rearrange("a p (h n) -> p (a h) n", h=QPG)).then_inc(wpraw_s, 16)
                    sp.wait_ge(w_ready, t + 1)
                    sp.dma_start(w_raw[:, :, :],
                                 wqkv[bass.ds(g + 1, 1), :, :].rearrange("a p (k n) -> p (a k) n", k=KH)).then_inc(wraw_s, 16)
            sp.wait_ge(t_done, (TURNS + 1) * NU)
            sp.wait_ge(prob_done, (TURNS + 1) * 32)
            sp.dma_start(had_sb, had_in.rearrange("p (a n) -> p a n", a=2)).then_inc(had_s, 16)
            sp.dma_start(raw_d, wdn.rearrange("p (m n) -> p m n", m=NM)).then_inc(rawd_s, 16)
            for n in range(4):
                if n:
                    sp.wait_ge(fly_s, 2 * n)
                sp.dma_start(raw, wug[n, :, :].rearrange("p (k n) -> p k n", k=KH)).then_inc(raw_s[0], 16)
            with sp.Fori(0, B * NC_B) as c:
                sp.wait_ge(fin_s, (c + 2) * 2)
                sp.dma_start(out[bass.ds(c * CT, CT), :, :].rearrange("t p n -> p t n"), o_out).then_inc(out_s, 16)
            sp.wait_ge(out_s, 16 * (B * NC_B + 1))

        @block.gpsimd
        def _(pool):
            g_ = nc.gpsimd
            pool.sem_inc(prob_done, per["prob_done"])
            pool.sem_inc(wp_ready, 1)
            g_.memset(mhalf[:, :], -0.5).then_inc(pool_self, 1)
            link = [1]

            def ln_rstd(r):
                with pool.Fori(0, B * NC_B) as q:
                    pool.wait_ge(ln[r]["vare"], q + 1)
                    g_.tensor_tensor(rstd[:, :], vare[:, :], mhalf[:, :], ALU.pow).then_inc(ln[r]["rstd"], 1)

            def split_w():
                g_.tensor_scalar(w_hi[:, :, :], w_raw[:, :, :], 1.0, 1.0, ALU.mult, ALU.mult).then_inc(pool_self, 1)

            pool.wait_ge(pool_self, 1)
            ln_rstd(0)
            pool.wait_ge(wraw_s, 16)
            split_w()
            pool.wait_ge(pool_self, 2)
            g_.tensor_tensor(w_lo[:, :, :], w_raw[:, :, :], w_hi[:, :, :].bitcast(F32), ALU.subtract).then_inc(w_ready, 1)
            pool.wait_ge(mod_ok, 1)
            with pool.Fori(0, B) as b:
                with pool.Fori(0, NKV) as g:
                    t = b * NKV + g
                    pool.wait_ge(wpraw_s, (t + 1) * 16)
                    g_.tensor_tensor(wp_raw[:, :, :], wp_raw[:, :, :],
                                     ga_row[:, bass.ds(b, 1), :].to_broadcast([P, QPG, HID]), ALU.mult).then_inc(pool_self, 1)
                    pool.wait_ge(y_done, this(y_done, t, 0))
                    pool.wait_ge(pool_self, t * 3 + 3)
                    pool.sem_inc(pool_gate, 1)
                    g_.tensor_scalar(wp_hi[:, :, :], wp_raw[:, :, :], 1.0, 1.0, ALU.mult, ALU.mult).then_inc(pool_self, 1)
                    pool.wait_ge(pool_self, t * 3 + 4)
                    g_.tensor_tensor(wp_lo[:, :, :], wp_raw[:, :, :], wp_hi[:, :, :].bitcast(F32), ALU.subtract).then_inc(wp_ready, 1)
                    for s, i in enumerate(STEPS):
                        for h in range(QPG):
                            e = QPG * s + h
                            pool.wait_ge(rinv_done, this(rinv_done, t, e + 1))
                            pool.sem_inc(pool_gate, 1)
                            row = prob[:, s % 2, h, 0:(i + 1) * P]
                            g_.tensor_scalar(row, row, rinv[:, s % 2, h:h + 1], 1.0, ALU.mult, ALU.mult).then_inc(prob_done, 1)
                        if s == 1:
                            pool.wait_ge(wraw_s, (t + 2) * 16)
                            pool.wait_ge(qkv_done, this(qkv_done, t, 12))
                            pool.sem_inc(pool_gate, 1)
                            split_w()
                            pool.wait_ge(pool_self, t * 3 + 5)
                            g_.tensor_tensor(w_lo[:, :, :], w_raw[:, :, :], w_hi[:, :, :].bitcast(F32),
                                             ALU.subtract).then_inc(w_ready, 1)
            ln_rstd(1)

        @block.scalar
        def _(act):
            a_ = nc.scalar
            for s, n in PER_ACT.items():
                act.sem_inc(s, n)
            act.dma_start(sc[:, 0, :, :], c_cols).then_inc(small_s, 16)
            act.dma_start(ident[:, :], ident_in).then_inc(small_s, 16)
            act.dma_start(mask_f[:, 0, :], mask_in).then_inc(small_s, 16)
            act.dma_start(wmod_sb, wmod.rearrange("(k p) n -> p k n", p=P)).then_inc(wmod_s, 16)
            act.dma_start(su_u[:, :], su_ug).then_inc(small_s, 16)
            act.dma_start(su_d[:, :], su_dp).then_inc(small_s, 16)
            act.dma_start(ws_u[:, :], ws_ug).then_inc(small_s, 16)
            act.dma_start(ws_d[:, :], ws_dp).then_inc(small_s, 16)
            act.wait_ge(small_s, 7 * 16)
            a_.activation(sc[:, 1, :, :], sc[:, 0, :, :], ACT.Exp, scale=-1.0).then_inc(silu_e, 1)

            def ln_modulate(r):
                shift, gain = (SA, CA) if r == 0 else (SB, CB)
                with act.Fori(0, B) as b:
                    with act.Fori(0, NC_B) as hf:
                        q = b * NC_B + hf
                        for k in range(KH):
                            act.wait_ge(ln[r]["lo"], q * KH + k + 1)
                            act.wait_ge(ln[r]["tr"], q * KH + k + 1)
                            act.wait_ge(mod_ok, 1)
                            a_.activation(h32[:, k, :], T[k], ACT.Identity,
                                          scale=cols[:, gain, k, bass.ds(b, 1)],
                                          bias=cols[:, shift, k, bass.ds(b, 1)]).then_inc(ln[r]["mod"], 1)

            ln_modulate(0)
            with act.Fori(0, B) as b:
                with act.Fori(0, NKV) as g:
                    t = b * NKV + g

                    def v_high():
                        for n in range(2):
                            act.wait_ge(vtr_done, this(vtr_done, t, n + 1))
                            a_.activation(v_hi[:, 4 * n:4 * n + 4, :].rearrange("p j d -> p (j d)"), T[n],
                                          ACT.Copy).then_inc(v_hi_s, 1)

                    for c, (what, h, half) in enumerate(CHUNKS):
                        act.wait_ge(qkv_done, this(qkv_done, t, c + 1))
                        span = slice(half * CH, (half + 1) * CH)
                        if what == "v":
                            a_.activation(vt[:, span], bank(c), ACT.Copy).then_inc(vt_done, 1)
                        elif what == "k":
                            a_.activation(k_hi[:, span], bank(c), ACT.Copy).then_inc(qkv_hi, 1)
                        else:
                            a_.activation(q_hi[:, h, span], bank(c), ACT.Copy, scale=SCALE).then_inc(qkv_hi, 1)
                        if c == V_AFTER + 1:
                            v_high()

                    waiting = []

                    def exps():
                        while waiting:
                            i, h = waiting.pop(0)
                            s = NT - 1 - i
                            nb, w = halves(i)
                            act.wait_ge(max_done, this(max_done, t, QPG * s + h + 1))
                            a_.activation(prob[:, s % 2, h, 0:nb * w].rearrange("p (a n) -> p a n", a=nb),
                                          S[h % 2][:, :].rearrange("p (a n) -> p a n", a=2)[:, 0:nb, 0:w],
                                          ACT.Exp, bias=nmax[:, s % 2, h:h + 1],
                                          accum_out=rsum[:, s % 2, h:h + 1]).then_inc(exp_done, 1)

                    for what, n, h in WALK:
                        if what == "S":
                            exps()
                            waiting.append((n, h))
                            if n == STEPS[0]:
                                exps()
                        if what == "T":
                            act.wait_ge(t_done, this(t_done, t, n + 1))
                            a_.activation(pt_hi[:, n % 3, :], T[n % 2], ACT.Copy).then_inc(pth_done, 1)
                            exps()
                        if what == "V" and n == LAST[UNITS[n][0]]:
                            s = NT - 1 - UNITS[n][0]
                            act.wait_ge(pv_done, this(pv_done, t, n + 1))
                            a_.activation(o_hi[:, s % 2, :], O, ACT.Copy).then_inc(oh_done, 1)

            ln_modulate(1)
            for n in range(4):
                for k in range(KH):
                    act.wait_ge(fmm_s, n * KH + k + 1)
                    a_.activation(wu_hi[:, k, n * CH:(n + 1) * CH], S[k][:, 0:CH], ACT.Identity,
                                  scale=su_u[:, k:k + 1]).then_inc(fhi_s, 1)
            for n in range(2):
                for k in range(KH):
                    act.wait_ge(fmm_s, (4 + n) * KH + k + 1)
                    for a in range(2):
                        m = n * 4 + k * 2 + a
                        a_.activation(wd_hi[n][:, m % 4, :], S[k][:, a * HID:(a + 1) * HID], ACT.Identity,
                                      scale=su_d[:, m:m + 1]).then_inc(fhi_s, 1)
            with act.Fori(0, B) as b:
                with act.Fori(0, NC_B) as hf:
                    c = b * NC_B + hf
                    for m in range(NM):
                        act.wait_ge(g32_s, c * NM + m + 1)
                        act.wait_ge(gu_s, c * NM + m + 1)
                        a_.activation(silu[:, m % 2, :], S[m % 2][:, 0:CH], ACT.Silu,
                                      scale=ws_u[:, NM + m:NM + m + 1]).then_inc(silu_s, 1)
                    for k in range(KH):
                        act.wait_ge(ytr_s, c * KH + 1)
                        act.wait_ge(dn_s, c * KH + k + 1)
                        act.wait_ge(mod_ok, 1)
                        a_.activation(yt[:, k, :], psum[3][:, k * CH:(k + 1) * CH], ACT.Identity,
                                      scale=cols[:, GB, k, bass.ds(b, 1)]).then_inc(yt_s, 1)

        @block.vector
        def _(dve):
            v_ = nc.vector
            for s, n in PER_DVE.items():
                dve.sem_inc(s, n)
            dve.sem_inc(ln[0]["lo"], KH)
            dve.sem_inc(ln[1]["lo"], KH)
            dve.sem_inc(g32_s, 2)
            dve.sem_inc(fin_s, 2)
            count = [0]

            def link(ins):
                count[0] += 1
                ins.then_inc(dve_self, 1)
                dve.wait_ge(dve_self, count[0])

            dve.wait_ge(silu_e, 1)
            v_.tensor_copy(ident_b[:, :], ident[:, :])
            v_.tensor_copy(mask_b[:, :], mask_f[:, 0, :])
            link(v_.tensor_scalar(sc[:, 2, :, :], sc[:, 1, :, :], 1.0, None, ALU.add))
            link(v_.reciprocal(sc[:, 3, :, :], sc[:, 2, :, :]))
            link(v_.tensor_tensor(sc[:, 1, :, :], sc[:, 0, :, :], sc[:, 3, :, :], ALU.mult))
            v_.tensor_copy(scb[:, :, :, :], sc[:, 1, :, :].unsqueeze(3).to_broadcast([P, KH, B, P])).then_inc(silu_c, 1)

            def guard(dst, tmp1, tmp2):
                link(v_.scalar_tensor_tensor(tmp1, dst, -1.0, dst, ALU.mult, ALU.max))
                link(v_.tensor_scalar(tmp1, tmp1, 0.25, None, ALU.max))
                link(v_.tensor_scalar(tmp2, dst, 0.0, 2.0, ALU.is_ge, ALU.mult))
                link(v_.scalar_tensor_tensor(dst, tmp2, -1.0, tmp1, ALU.add, ALU.mult))

            def modulation():
                dve.wait_ge(mod_mm, 1)
                link(v_.tensor_copy(cols[:, :, :, :], Y[:, 0:24].rearrange("p (v k b) -> p v k b", v=6, k=KH)))
                for v in (CA, CB):
                    link(v_.tensor_scalar(cols[:, v, :, :], cols[:, v, :, :], 1.0, None, ALU.add))
                guard(cols[:, GB, :, :], sc[:, 2, :, :], sc[:, 3, :, :])
                link(v_.tensor_tensor(cols[:, GB, :, :], cols[:, GB, :, :],
                                      ws_d[:, :].unsqueeze(2).to_broadcast([P, KH, B]), ALU.mult))
                link(v_.tensor_copy(ga_row[:, :, :], O[:, 0:B * HID].rearrange("p (b n) -> p b n", b=B)))
                guard(ga_row[:, :, :], guard_a, guard_b)
    
            def ln_chunk(r, q):
                s = ln[r]
                for j in range(CT):
                    v_.bn_stats(stats[:, j, :], x[:, bass.ds(q * CT + j, 1), :].rearrange("p a n -> p (a n)")).then_inc(s["stats"], 1)
                for j in range(CT):
                    dve.wait_ge(s["stats"], q * CT + j + 1)
                    dve.sem_inc(dve_gate, 1)
                    v_.bn_aggr(mv[:, j, :], stats[:, j, :]).then_inc(s["aggr"], 1)
                dve.wait_ge(s["aggr"], q * CT + CT)
                v_.tensor_scalar(vare[:, :], mv[:, :, 1], EPS, None, ALU.add).then_inc(s["vare"], 1)
                dve.wait_ge(s["rstd"], q + 1)
                for j in range(CT):
                    v_.tensor_scalar(xhat[:, j, :], x[:, bass.ds(q * CT + j, 1), :].rearrange("p a n -> p (a n)"),
                                     mv[:, j, 0:1], rstd[:, j:j + 1], ALU.subtract, ALU.mult).then_inc(s["xhat"], 1)

            def ln_parts(r, q, hi, lo):
                s = ln[r]
                for k in range(KH):
                    dve.wait_ge(s["mod"], q * KH + k + 1)
                    v_.tensor_copy(hi[:, k, bass.ds(q * CH, CH)], h32[:, k, :]).then_inc(s["hi"], 1)
                    dve.wait_ge(s["hi"], q * KH + k + 1)
                    v_.tensor_tensor(lo[:, k, bass.ds(q * CH, CH)], h32[:, k, :],
                                     hi[:, k, bass.ds(q * CH, CH)].bitcast(F32), ALU.subtract).then_inc(s["lo"], 1)

            modulation()
            v_.tensor_copy(sc[:, 2, :, :], sc[:, 3, :, :]).then_inc(mod_ok, 1)
            with dve.Fori(0, B * NC_B) as q:
                dve.wait_ge(x_in_s, B * NC_B * 16)
                ln_chunk(0, q)
                ln_parts(0, q, h_hi, h_lo)

            with dve.Fori(0, B) as b:
                with dve.Fori(0, NKV) as g:
                    t = b * NKV + g
                    low = 0
                    for c, (what, h, half) in enumerate(CHUNKS):
                        span = slice(half * CH, (half + 1) * CH)
                        if what != "v":
                            low += 1
                            dve.wait_ge(qkv_hi, this(qkv_hi, t, low))
                            if what == "k":
                                v_.tensor_tensor(k_lo[:, span], bank(c), k_hi[:, span].bitcast(F32),
                                                 ALU.subtract).then_inc(qkv_lo, 1)
                            else:
                                v_.scalar_tensor_tensor(q_lo[:, h, span], bank(c), SCALE, q_hi[:, h, span].bitcast(F32),
                                                        ALU.mult, ALU.subtract).then_inc(qkv_lo, 1)
                        if c == V_AFTER + 1:
                            for n in range(2):
                                dve.wait_ge(v_hi_s, this(v_hi_s, t, n + 1))
                                v_.tensor_tensor(v_lo[:, 4 * n:4 * n + 4, :].rearrange("p j d -> p (j d)"), T[n],
                                                 v_hi[:, 4 * n:4 * n + 4, :].rearrange("p j d -> p (j d)").bitcast(F32),
                                                 ALU.subtract).then_inc(v_lo_s, 1)

                    waiting = []

                    def inverse():
                        while waiting:
                            i, h = waiting.pop(0)
                            s = NT - 1 - i
                            dve.wait_ge(exp_done, this(exp_done, t, QPG * s + h + 1))
                            v_.reciprocal(rinv[:, s % 2, h:h + 1], rsum[:, s % 2, h:h + 1]).then_inc(rinv_done, 1)

                    for what, n, h in WALK:
                        if what == "S":
                            s = NT - 1 - n
                            nb, w = halves(n)
                            dve.wait_ge(s_done, this(s_done, t, QPG * s + h + 1))
                            v_.tensor_reduce(nmax[:, s % 2, h:h + 1],
                                             S[h % 2][:, :].rearrange("p (a n) -> p a n", a=2)[:, 0:nb, 0:w],
                                             AX.XY, ALU.max, negate=True).then_inc(max_done, 1)
                            inverse()
                            waiting.append((n, h))
                        if what == "T":
                            dve.wait_ge(pth_done, this(pth_done, t, n + 1))
                            v_.tensor_tensor(pt_lo[:, n % 3, :], T[n % 2], pt_hi[:, n % 3, :].bitcast(F32),
                                             ALU.subtract).then_inc(ptl_done, 1)
                            inverse()
                        if what == "V" and n == LAST[UNITS[n][0]]:
                            s = NT - 1 - UNITS[n][0]
                            dve.wait_ge(oh_done, this(oh_done, t, s + 1))
                            v_.tensor_tensor(o_lo[:, s % 2, :], O, o_hi[:, s % 2, :].bitcast(F32),
                                             ALU.subtract).then_inc(ol_done, 1)
                        if what == "Y":
                            s = NT - 1 - n
                            dve.wait_ge(y_done, this(y_done, t, s + 1))
                            row = x[:, bass.ds(b * NT + n, 1), :].rearrange("p a n -> p (a n)")
                            v_.tensor_tensor(row, Y[:, 0:HID], row, ALU.add).then_inc(add_done, 1)

            dve.wait_ge(t_done, (TURNS + 1) * NU)
            dve.wait_ge(add_done, (TURNS + 1) * NT)
            with dve.Fori(0, B * NC_B) as q:
                ln_chunk(1, q)
                ln_parts(1, q, h2_hi, h2_lo)
            dve.wait_ge(had_s, 16)
            dve.wait_ge(w_ready, TURNS + 1)
            v_.tensor_copy(had_r, had_sb).then_inc(had_ok, 1)

            def flown(n, src):
                link(v_.tensor_copy(fly_hi, src))
                v_.tensor_tensor(fly_lo, src, fly_hi.bitcast(F32), ALU.subtract).then_inc(fly_ok, 1)

            for n in range(4):
                dve.wait_ge(raw_s[0], 16 * (n + 1))
                v_.tensor_tensor(fly[:, 0, :], raw[:, 0, :], raw[:, 1, :], ALU.add).then_inc(fly_s, 1)
                v_.tensor_tensor(fly[:, 1, :], raw[:, 0, :], raw[:, 1, :], ALU.subtract).then_inc(fly_s, 1)
                dve.wait_ge(fly_s, 2 * (n + 1))
                if n:
                    dve.wait_ge(fmm_s, n * KH)
                flown(n, fly)
                for k in range(KH):
                    dve.wait_ge(fhi_s, n * KH + k + 1)
                    v_.scalar_tensor_tensor(wu_lo[:, k, n * CH:(n + 1) * CH], S[k][:, 0:CH], su_u[:, k:k + 1],
                                            wu_hi[:, k, n * CH:(n + 1) * CH].bitcast(F32),
                                            ALU.mult, ALU.subtract).then_inc(wf_ok, 1)
            dve.wait_ge(rawd_s, 16)
            src, dst = raw_d, raw_d2
            for bit in range(3):
                a = src.rearrange("p (u two v) n -> p u two (v n)", two=2, v=1 << bit)
                z = dst.rearrange("p (u two v) n -> p u two (v n)", two=2, v=1 << bit)
                v_.tensor_tensor(z[:, :, 0, :], a[:, :, 0, :], a[:, :, 1, :], ALU.add)
                link(v_.tensor_tensor(z[:, :, 1, :], a[:, :, 0, :], a[:, :, 1, :], ALU.subtract))
                src, dst = dst, src
            for n in range(2):
                dve.wait_ge(fmm_s, (4 + n) * KH)
                flown(4 + n, src[:, 4 * n:4 * n + 4, :].rearrange("p m n -> p (m n)").rearrange("p (k n) -> p k n", k=KH))
                for k in range(KH):
                    dve.wait_ge(fhi_s, 8 + n * 4 + k * 2 + 2)
                    for a in range(2):
                        m = n * 4 + k * 2 + a
                        v_.scalar_tensor_tensor(wd_lo[n][:, m % 4, :], S[k][:, a * HID:(a + 1) * HID], su_d[:, m:m + 1],
                                                wd_hi[n][:, m % 4, :].bitcast(F32), ALU.mult, ALU.subtract).then_inc(wf_ok, 1)
            with dve.Fori(0, B * NC_B) as c:
                for m in range(NM):
                    dve.wait_ge(silu_s, c * NM + m + 1)
                    v_.scalar_tensor_tensor(g32[:, m % 2, :], S[m % 2][:, CH:2 * CH], ws_u[:, m:m + 1], silu[:, m % 2, :],
                                            ALU.mult, ALU.mult).then_inc(g32_s, 1)
                    dve.wait_ge(g32_s, c * NM + m + 3)
                    v_.tensor_copy(g_hi[:, m % 3, :], g32[:, m % 2, :]).then_inc(ghi_s, 1)
                    dve.wait_ge(ghi_s, c * NM + m + 1)
                    v_.tensor_tensor(g_lo[:, m % 3, :], g32[:, m % 2, :], g_hi[:, m % 3, :].bitcast(F32),
                                     ALU.subtract).then_inc(g_ok, 1)
                dve.wait_ge(out_s, (c + 1) * 16)
                for a in range(2):
                    dve.wait_ge(ytr_s, (c + 1) * KH + a + 1)
                    v_.tensor_tensor(o_out[:, 2 * a:2 * a + 2, :], T[a].rearrange("p (j n) -> p j n", j=2),
                                     x[:, bass.ds(c * CT + 2 * a, 2), :], ALU.add).then_inc(fin_s, 1)

        @block.tensor
        def _(pe):
            mm, tr = nc.tensor.matmul, nc.tensor.transpose
            for s, n in PER_PE.items():
                pe.sem_inc(s, n)
            pe.sem_inc(ytr_s, KH)

            def three(dst, w_h, w_l, r_h, r_l, start, stop):
                mm(dst, w_h, r_h, start=start, stop=False)
                mm(dst, w_h, r_l, start=False, stop=False)
                return mm(dst, w_l, r_h, start=False, stop=stop)

            pe.wait_ge(silu_c, 1)
            pe.wait_ge(wmod_s, 16)
            for v in range(6):
                for k in range(KH):
                    for a in range(KH):
                        at = (v * KH + k) * B
                        mm(Y[:, at:at + B], wmod_sb[:, a, v * HID + k * P:v * HID + (k + 1) * P], sc[:, 1, a, :],
                           start=a == 0, stop=a == KH - 1)
            for b in range(B):
                for a in range(KH):
                    last = mm(O[:, b * HID:(b + 1) * HID], scb[:, a, b, :], wmod_sb[:, a, GA * HID:(GA + 1) * HID],
                              start=a == 0, stop=a == KH - 1)
            last.then_inc(mod_mm, 1)

            def ln_transpose(r):
                s = ln[r]
                with pe.Fori(0, B * NC_B) as q:
                    for k in range(KH):
                        pe.wait_ge(s["lo"], q * KH + k + 1)
                        for j in range(CT):
                            if k == 0:
                                pe.wait_ge(s["xhat"], q * CT + j + 1)
                            last = tr(T[k][:, j * P:(j + 1) * P], xhat[:, j, k * P:(k + 1) * P], ident[:, :])
                        last.then_inc(s["tr"], 1)

            ln_transpose(0)
            pe.wait_ge(ln[0]["lo"], (B * NC_B + 1) * KH)
            with pe.Fori(0, B) as b:
                with pe.Fori(0, NKV) as g:
                    t = b * NKV + g
                    for c, (what, h, half) in enumerate(CHUNKS):
                        if c == 0:
                            pe.wait_ge(exp_done, this(exp_done, t, 0))
                            pe.wait_ge(w_ready, t + 1)
                        elif c in (4, 5):
                            pe.wait_ge(vt_done, this(vt_done, t, c - 3))
                        elif c >= 6:
                            pe.wait_ge(qkv_lo, this(qkv_lo, t, c - 5))
                        at = {"q": h, "k": QPG, "v": QPG + 1}[what] * D
                        for k in range(KH):
                            cols_h = bass.ds(b * SEQ + half * CH, CH)
                            last = three(bank(c), w_hi[:, k, at:at + D], w_lo[:, k, at:at + D],
                                         h_hi[:, k, cols_h], h_lo[:, k, cols_h], k == 0, k == KH - 1)
                        last.then_inc(qkv_done, 1)
                        if c == V_AFTER:
                            pe.wait_ge(ptl_done, this(ptl_done, t, 0))
                            for n in range(2):
                                pe.wait_ge(vt_done, this(vt_done, t, n + 1))
                                for j in range(4):
                                    last = tr(T[n][:, j * P:(j + 1) * P], vt[:, (4 * n + j) * P:(4 * n + j + 1) * P], ident[:, :])
                                last.then_inc(vtr_done, 1)

                    for what, n, h in WALK:
                        if what == "S":
                            s = NT - 1 - n
                            e = QPG * s + h
                            if e < 2:
                                pe.wait_ge(qkv_lo, this(qkv_lo, t, 8 + 2 * e))
                            else:
                                pe.wait_ge(exp_done, this(exp_done, t, e - 1))
                            nb, w = halves(n)
                            wide = max(w, 2 * P)
                            q_at = slice(n * P, (n + 1) * P)
                            for a in range(nb):
                                mm(S[h % 2][:, a * CH:a * CH + wide], q_hi[:, h, q_at], k_hi[:, a * w:a * w + wide],
                                   start=True, stop=False)
                            at = (nb - 1) * CH + w - P
                            mm(S[h % 2][:, at:at + P], ident_b[:, :], mask_b[:, :], start=False, stop=False)
                            for a in range(nb):
                                mm(S[h % 2][:, a * CH:a * CH + wide], q_hi[:, h, q_at], k_lo[:, a * w:a * w + wide],
                                   start=False, stop=False)
                            for a in range(nb):
                                last = mm(S[h % 2][:, a * CH:a * CH + wide], q_lo[:, h, q_at], k_hi[:, a * w:a * w + wide],
                                          start=False, stop=True)
                            last.then_inc(s_done, 1)
                        if what == "T":
                            i, j = UNITS[n]
                            s = NT - 1 - i
                            if n >= 2:
                                pe.wait_ge(ptl_done, this(ptl_done, t, n - 1))
                            else:
                                pe.wait_ge(v_lo_s, this(v_lo_s, t, n + 1))
                            for h in range(QPG):
                                if j == 0:
                                    pe.wait_ge(prob_done, this(prob_done, t, QPG * s + h + 1))
                                last = tr(T[n % 2][:, h * P:(h + 1) * P], prob[:, s % 2, h, j * P:(j + 1) * P], ident[:, :])
                            last.then_inc(t_done, 1)
                        if what == "V":
                            i, j = UNITS[n]
                            s = NT - 1 - i
                            if j == 0:
                                pe.wait_ge(ol_done, this(ol_done, t, s))
                            if n == 0:
                                pe.wait_ge(v_lo_s, this(v_lo_s, t, 2))
                            pe.wait_ge(ptl_done, this(ptl_done, t, n + 1))
                            three(O, v_hi[:, j, :], v_lo[:, j, :], pt_hi[:, n % 3, :], pt_lo[:, n % 3, :],
                                  j == 0, j == i).then_inc(pv_done, 1)
                        if what == "Y":
                            s = NT - 1 - n
                            if s == 0:
                                pe.wait_ge(wp_ready, t + 2)
                            pe.wait_ge(add_done, this(add_done, t, s))
                            pe.wait_ge(ol_done, this(ol_done, t, s + 1))
                            for h in range(QPG):
                                last = three(Y[:, 0:HID], o_hi[:, s % 2, h * P:(h + 1) * P], o_lo[:, s % 2, h * P:(h + 1) * P],
                                             wp_hi[:, h, :], wp_lo[:, h, :], h == 0, h == QPG - 1)
                            last.then_inc(y_done, 1)

            ln_transpose(1)
            pe.wait_ge(had_ok, 1)
            for n in range(6):
                pe.wait_ge(fly_ok, n + 1)
                if n:
                    pe.wait_ge(wf_ok, KH * n if n <= 4 else 8 + 4)
                for k in range(KH):
                    mm(S[k][:, 0:CH], had_r[:, n // 4, :], fly_hi[:, k, :], start=True, stop=False)
                    mm(S[k][:, 0:CH], had_r[:, n // 4, :], fly_lo[:, k, :], start=False, stop=True).then_inc(fmm_s, 1)
            pe.wait_ge(wf_ok, 8 + NM)
            pe.wait_ge(ln[1]["lo"], (B * NC_B + 1) * KH)
            with pe.Fori(0, B * NC_B) as c:

                def down(m):
                    pe.wait_ge(g_ok, c * NM + m + 1)
                    for k in range(KH):
                        last = three(psum[3][:, k * CH:(k + 1) * CH],
                                     wd_hi[m // 4][:, m % 4, k * P:(k + 1) * P], wd_lo[m // 4][:, m % 4, k * P:(k + 1) * P],
                                     g_hi[:, m % 3, :], g_lo[:, m % 3, :], m == 0, m == NM - 1)
                        if m == NM - 1:
                            last.then_inc(dn_s, 1)

                for m in range(NM):
                    pe.wait_ge(g32_s, c * NM + m + 1)
                    for a, at in ((0, INTER + m * P), (1, m * P)):
                        for k in range(KH):
                            last = three(S[m % 2][:, a * CH:(a + 1) * CH], wu_hi[:, k, at:at + P], wu_lo[:, k, at:at + P],
                                         h2_hi[:, k, bass.ds(c * CH, CH)], h2_lo[:, k, bass.ds(c * CH, CH)],
                                         k == 0, k == KH - 1)
                    last.then_inc(gu_s, 1)
                    if m:
                        down(m - 1)
                down(NM - 1)
                pe.wait_ge(yt_s, (c + 1) * KH)
                for a in range(2):
                    pe.wait_ge(fin_s, c * 2 + a + 1)
                    for j in range(2):
                        for k in range(KH):
                            last = tr(T[a][:, j * HID + k * P:j * HID + (k + 1) * P],
                                      yt[:, k, (2 * a + j) * P:(2 * a + j + 1) * P], ident[:, :])
                    last.then_inc(ytr_s, 1)


def kernel(**inputs):
    import concourse.bacc as bacc
    from concourse.bass_utils import run_bass_kernel_spmd

    def get(name):
        return np.asarray(inputs[name])

    x = np.ascontiguousarray(get("L0_attn_x").reshape(B * NT, P, HID))
    w = get("L0_attn_weight_qkv").reshape(NKV, GW, KH, P).transpose(0, 3, 2, 1).reshape(NKV, P, KH * GW)
    w = np.concatenate([w, w[:1]])
    wp = get("L0_attn_weight_proj").reshape(HID, NKV, QPG, D).transpose(1, 3, 2, 0).reshape(NKV, P, QPG * HID)
    up_gate = np.concatenate([get("L0_ffn_W_up"), get("L0_ffn_W_gate")])
    wug = up_gate.reshape(4, CH, KH, P).transpose(0, 3, 2, 1).reshape(4, P, KH * CH)
    wdn = get("L0_ffn_W_down").reshape(HID, NM, P).transpose(2, 1, 0).reshape(P, NM * HID)
    n = np.arange(P)
    had = np.array([[1.0]])
    while len(had) < P:
        had = np.block([[had, had], [had, -had]])
    had = np.concatenate([had / HID ** 0.5, had / INTER ** 0.5], axis=1).astype(np.float32)
    arrays = {
        "x": x, "wqkv": w, "wproj": wp, "wmod": get("L0_wmod"),
        "c": get("L0_c").reshape(B, KH, P).transpose(2, 1, 0), "wug": wug, "wdn": wdn,
        "su_ug": get("L0_ffn_SU_ug").reshape(KH, P).T, "su_dp": get("L0_ffn_SU_dp").reshape(NM, P).T,
        "ws_ug": get("L0_ffn_Wscale_ug").reshape(2 * NM, P).T, "ws_dp": get("L0_ffn_Wscale_dp").reshape(KH, P).T,
        "ident": np.eye(P, dtype=np.float32),
        "mask": np.where(n[None, :] > n[:, None], MASKED, 0.0).astype(np.float32), "had": had,
    }
    nc = bacc.Bacc("TRN2", target_bir_lowering=False, num_devices=1)
    feed, args = {}, []
    for name, a in arrays.items():
        a = np.ascontiguousarray(a)
        feed[f"in_{name}"] = a
        args.append(nc.dram_tensor(f"in_{name}", a.shape, mybir.dt.from_np(a.dtype), kind="ExternalInput").ap())
    args.append(nc.dram_tensor("out_y", (B * NT, P, HID), F32, kind="ExternalOutput").ap())
    build(nc, *args)
    r = run_bass_kernel_spmd(nc, [feed], core_ids=[0])
    return r.results[0]["out_y"].reshape(B, SEQ, HID)
```

```python
import numpy as np
import concourse.bass as bass
from concourse import mybir
from contextlib import ExitStack

F32 = mybir.dt.float32
F32R = mybir.dt.float32r
BF16 = mybir.dt.bfloat16
ALU = mybir.AluOpType
ACT = mybir.ActivationFunctionType
AX = mybir.AxisListType

P = 128
B, SEQ, HID = 2, 1024, 256
NKV, QPG, D = 4, 4, 128
INTER = 1024
KH = HID // P
NT = SEQ // P
NM = INTER // P
CH = 512
CT = CH // P
NC_B = SEQ // CH
LP = 2
NP = NT // LP
GW = (QPG + 2) * D
SCALE = float(D) ** -0.5
EPS = 1e-5
MASKED = -1e30
STEPS = [NT - 1 - s for s in range(NT)]
UNITS = [(i, j) for i in STEPS for j in range(i + 1)]
NU = len(UNITS)
LAST = {i: max(n for n, u in enumerate(UNITS) if u[0] == i) for i in STEPS}
SA, CA, GA, SB, CB, GB = range(6)


def walk():
    out = [("C", c, 0) for c in range(6)] + [("VT", 0, 0), ("C", 6, 0), ("C", 7, 0)]
    for h in range(QPG):
        out += [("S", STEPS[0], h), ("C", 8 + h, 0)]
    lag = 2

    def values(n):
        out.append(("V", n, 0))
        i, j = UNITS[n]
        if i < STEPS[0] and j == min(1, i):
            out.append(("Y", i + 1, 0))

    for n, (i, j) in enumerate(UNITS):
        for h in range(QPG):
            if i and j == h * (i + 1) // (QPG + 1):
                out.append(("S", i - 1, h))
        out.append(("T", n, 0))
        if n >= lag:
            values(n - lag)
        if n == 3:
            out.append(("L", 0, 0))
    for n in range(NU - lag, NU):
        values(n)
    out.append(("Y", 0, 0))
    return out


WALK = walk()


def halves(i):
    n = (i + 1) * P
    return (2, n // 2) if n > CH else (1, n)


def build(nc, x_in, wqkv, wproj, wmod, c_cols, wug, wdn, su_ug, su_dp, ws_ug, ws_dp, ident_in, mask_in, had_in, out):
    ctx = ExitStack()
    with ctx:
        def sb(name, shape, dt=F32):
            return ctx.enter_context(nc.sbuf_tensor(name, shape, dt))

        def sem(name):
            return ctx.enter_context(nc.semaphore(name))

        x = sb("x", [P, B * NT, HID])
        h_hi = sb("h_hi", [P, KH, B * SEQ], F32R)
        h_lo = sb("h_lo", [P, KH, B * SEQ], F32R)
        q_hi = sb("q_hi", [P, QPG, SEQ], F32R)
        q_lo = sb("q_lo", [P, QPG, SEQ], F32R)
        k_hi = sb("k_hi", [P, SEQ], F32R)
        k_lo = sb("k_lo", [P, SEQ], F32R)
        v_hi = sb("v_hi", [P, NT, D], F32R)
        v_lo = sb("v_lo", [P, NT, D], F32R)
        prob = sb("prob", [P, 2, QPG, SEQ])
        pt_hi = sb("pt_hi", [P, 3, CH], F32R)
        pt_lo = sb("pt_lo", [P, 3, CH], F32R)
        o_hi = sb("o_hi", [P, 2, CH], F32R)
        o_lo = sb("o_lo", [P, 2, CH], F32R)
        w_raw = sb("w_raw", [P, KH, GW])
        w_hi = sb("w_hi", [P, KH, GW], F32R)
        w_lo = sb("w_lo", [P, KH, GW], F32R)
        wp_raw = sb("wp_raw", [P, QPG, HID])
        wp_hi = sb("wp_hi", [P, QPG, HID], F32R)
        wp_lo = sb("wp_lo", [P, QPG, HID], F32R)
        ga_row = sb("ga_row", [P, B, HID])
        cols = sb("cols", [P, 6, KH, B])
        ident = sb("ident", [P, P])
        ident_b = sb("ident_b", [P, P], BF16)
        mask_b = sb("mask_b", [P, P], BF16)
        nmax = sb("nmax", [P, 2, QPG])
        rsum = sb("rsum", [P, 2, QPG])
        rinv = sb("rinv", [P, 2, QPG])
        xhat0 = sb("xhat", [P, LP, HID])
        h320 = sb("h32", [P, KH, LP * P])
        stats = sb("stats", [P, 2, LP, 6])
        mv = sb("mv", [P, 2, LP, 2])
        vare = sb("vare", [P, 2, LP])
        rstd = sb("rstd", [P, 2, LP])
        mhalf = sb("mhalf", [P, LP])
        su_u = sb("su_u", [P, KH])
        su_d = sb("su_d", [P, NM])
        ws_u = sb("ws_u", [P, 2 * NM])
        ws_d = sb("ws_d", [P, KH])
        sc = sb("sc", [P, 4, KH, B])
        scb = sb("scb", [P, KH, B, P])

        flat = prob[:, :, :, :].rearrange("p a h n -> p (a h n)")

        def part(start, *shape):
            size = int(np.prod(shape))
            names = "abcd"[:len(shape)]
            return flat[:, start:start + size].rearrange(
                f"p ({' '.join(names)}) -> p {' '.join(names)}", **dict(zip(names, shape)))

        vt = prob[:, 1, 0, :]
        xhat = [xhat0, part(0, LP, HID)]
        h32 = [h320, part(512, KH, LP * P)]
        wmod_sb = part(1024, KH, 6 * HID)
        mask_f = part(4096, 1, P)
        guard_a, guard_b = part(4224, B, HID), part(4736, B, HID)
        had_f = part(1024, 2, 2 * P)
        raw = [part(1536 + n * KH * CH, KH, CH) for n in range(6)]
        raw_all_dn = flat[:, 1536 + 4 * KH * CH:1536 + 6 * KH * CH]
        raw_dn = flat[:, 1536 + 4 * KH * CH:1536 + 6 * KH * CH].rearrange("p (a k o n) -> p a k o n", a=2, k=KH, o=2)
        sum_dn, dif_dn = (a.rearrange("p k n -> p (k n)")[:, 0:4 * HID].rearrange("p (a k n) -> p a k n", a=2, k=KH)
                          for a in (w_raw[:, :, :], wp_raw[:, :, :]))
        g32 = part(2048, 2, CH)
        silu = part(3072, 2, CH)
        yt = part(4096, KH, CH)
        o_out = part(5120, CT, HID)
        had_r = [w_hi[:, 0, CH:CH + 2 * P], w_hi[:, 1, CH:CH + 2 * P]]
        raw_hi = [w_hi[:, :, 0:CH], o_hi[:, :, :]]
        raw_lo = [w_lo[:, :, 0:CH], o_lo[:, :, :]]
        wu_hi = q_hi[:, :, :].rearrange("p (k b) n -> p k (b n)", k=KH)
        wu_lo = q_lo[:, :, :].rearrange("p (k b) n -> p k (b n)", k=KH)
        wd_hi = [a[:, :].rearrange("p (m n) -> p m n", m=4) for a in (k_hi, k_lo)]
        wd_lo = [a[:, :, :].rearrange("p m d -> p (m d)").rearrange("p (m n) -> p m n", m=4) for a in (v_hi, v_lo)]
        g_hi, g_lo = pt_hi, pt_lo

        psum = [ctx.enter_context(nc.psum_tensor(f"ps{n}", [P, 2 * CH], F32)) for n in range(4)]
        S = [psum[0], psum[1]]
        T = [psum[2][:, 0:CH], psum[2][:, CH:2 * CH]]
        X = [psum[3][:, 0:CH], psum[3][:, CH:2 * CH]]

        x_in_s = [sem(f"x_loaded{b}") for b in range(B)]
        small_s = sem("small_loaded")
        wmod_s = sem("wmod_loaded")
        wraw_s = sem("w_raw_loaded")
        wpraw_s = sem("wp_raw_loaded")
        consts = sem("constants_made")
        silu_e = sem("mod_exp")
        silu_c = sem("mod_silu")
        mod_mm = sem("mod_multiplied")
        mod_ok, gate_ok = sem("mod_ready"), sem("gate_ready")
        dve_self = sem("dve_self")
        pool_self = sem("pool_self")
        dve_gate, act_gate, pool_gate = sem("dve_gate"), sem("act_gate"), sem("pool_gate")
        ln = [{k: sem(f"ln{r}_{k}") for k in ("stats", "aggr", "vare", "rstd", "xhat", "tr", "hi", "lo")} for r in range(3)]
        LN_SLOTS = [2, 1, 2]
        qkv_done, qkv_hi, qkv_lo = sem("qkv_done"), sem("qkv_hi"), sem("qkv_lo")
        vt_done, vtr_done, v_hi_s, v_lo_s = sem("vt_done"), sem("vtr_done"), sem("v_hi_done"), sem("v_lo_done")
        s_done, max_done, exp_done = sem("scores_done"), sem("max_done"), sem("exp_done")
        rinv_done, prob_done = sem("rinv_done"), sem("prob_done")
        t_done, pth_done, ptl_done = sem("transposed"), sem("pt_hi_done"), sem("pt_lo_done")
        pv_done, oh_done, ol_done = sem("pv_done"), sem("o_hi_done"), sem("o_lo_done")
        y_done, add_done = sem("y_done"), sem("x_added")
        w_ready, wp_ready = sem("w_ready"), sem("wp_ready")
        raw_s = [sem(f"raw_loaded{n}") for n in range(5)]
        had_s, had_ok, fly_s = sem("had_loaded"), sem("had_ready"), sem("butterflies")
        rhi_s, rlo_s, fmm_s, fhi_s, wf_ok = (sem("raw_hi_done"), sem("raw_lo_done"), sem("hadamard_done"),
                                             sem("wf_hi"), sem("wf_ready"))
        gu_s, silu_s, g32_s, ghi_s, g_ok = sem("gate_up_done"), sem("silu_done"), sem("g32_done"), sem("g_hi_done"), sem("g_ready")
        dn_s, yt_s, ytr_s, fin_s, out_s = sem("down_done"), sem("yt_done"), sem("y_transposed"), sem("out_ready"), sem("out_stored")

        PER_PE = {qkv_done: 12, vtr_done: 2, s_done: 32, t_done: NU, pv_done: NU, y_done: NT}
        PER_ACT = {qkv_hi: 10, vt_done: 2, v_hi_s: 2, exp_done: 32, pth_done: NU, oh_done: NT}
        PER_DVE = {qkv_lo: 10, v_lo_s: 2, max_done: 32, rinv_done: 32, ptl_done: NU, ol_done: NT, add_done: NT}
        PER_POOL = {prob_done: 32}
        per = {s.name: n for d in (PER_PE, PER_ACT, PER_DVE, PER_POOL) for s, n in d.items()}
        TURNS = B * NKV

        def this(s, t, k):
            return (t + 1) * per[s.name] + k

        CHUNKS = [("v", 0, 0), ("v", 0, 1), ("k", 0, 0), ("k", 0, 1)]
        CHUNKS += [("q", h, 1) for h in range(QPG)] + [("q", h, 0) for h in range(QPG)]

        def bank(c):
            return psum[c % 4 // 2][:, c % 2 * CH:(c % 2 + 1) * CH] if c < 8 else X[c % 2]

        def ln_step(r, b, g, slot):
            if r == 1:
                return b * NKV + g, b * -NT + g * LP + NT, b * -1 + 1, b
            return g * 2 + slot, (r // 2) * NT + (g * 2 + slot) * LP, r // 2, r // 2

        ln_bank = [T, [X[1]], T]

        block = ctx.enter_context(nc.Block())

        @block.sync
        def _(sp):
            sp.sem_inc(out_s, 16)
            def load_x(c):
                sp.dma_start(x[:, c * CT:(c + 1) * CT, :],
                             x_in[c * CT:(c + 1) * CT, :, :].rearrange("t p n -> p t n")).then_inc(x_in_s[c // NC_B], 16)

            load_x(0)
            load_x(1)
            sp.dma_start(wmod_sb, wmod.rearrange("(k p) n -> p k n", p=P)).then_inc(wmod_s, 16)
            sp.dma_start(w_raw[:, :, :], wqkv[0, :, :].rearrange("p (k n) -> p k n", k=KH)).then_inc(wraw_s, 16)
            load_x(2)
            load_x(3)
            with sp.Fori(0, B) as b:
                with sp.Fori(0, NKV) as g:
                    t = b * NKV + g
                    sp.wait_ge(wp_ready, t + 1)
                    sp.dma_start(wp_raw[:, :, :],
                                 wproj[bass.ds(g, 1), :, :].rearrange("a p (h n) -> p (a h) n", h=QPG)).then_inc(wpraw_s, 16)
                    sp.wait_ge(w_ready, t + 1)
                    sp.dma_start(w_raw[:, :, :],
                                 wqkv[bass.ds(g + 1, 1), :, :].rearrange("a p (k n) -> p (a k) n", k=KH)).then_inc(wraw_s, 16)
            sp.wait_ge(t_done, (TURNS + 1) * NU)
            sp.wait_ge(prob_done, (TURNS + 1) * 32)
            sp.dma_start(had_f, had_in.rearrange("p (a n) -> p a n", a=2)).then_inc(had_s, 16)
            for n in (0, 1, 4, 2, 3):
                if n < 4:
                    sp.dma_start(raw[n], wug[n, :, :].rearrange("p (k n) -> p k n", k=KH)).then_inc(raw_s[n], 16)
                else:
                    sp.dma_start(raw_all_dn, wdn).then_inc(raw_s[n], 16)
            with sp.Fori(0, B * NC_B) as c:
                sp.wait_ge(fin_s, (c + 2) * 2)
                sp.dma_start(out[bass.ds(c * CT, CT), :, :].rearrange("t p n -> p t n"), o_out).then_inc(out_s, 16)
            sp.wait_ge(out_s, 16 * (B * NC_B + 1))

        @block.gpsimd
        def _(pool):
            g_ = nc.gpsimd
            pool.sem_inc(prob_done, per["prob_done"])
            pool.sem_inc(wp_ready, 1)
            g_.memset(mhalf[:, :], -0.5).then_inc(pool_self, 1)
            link = [1]

            def ln_rstd(r, b, g, slot):
                n = ln_step(r, b, g, slot)[0]
                pool.wait_ge(ln[r]["vare"], n + 1)
                g_.tensor_tensor(rstd[:, slot, :], vare[:, slot, :], mhalf[:, :], ALU.pow).then_inc(ln[r]["rstd"], 1)

            def ln_low(r, b, g, slot):
                n, block, _, _ = ln_step(r, b, g, slot)
                pool.wait_ge(ln[r]["hi"], n + LN_SLOTS[r] + 1)
                at = bass.ds(block * P, LP * P)
                g_.tensor_tensor(h_lo[:, :, at], h32[slot][:, :, :], h_hi[:, :, at].bitcast(F32), ALU.subtract).then_inc(ln[r]["lo"], 1)

            def split_w():
                g_.tensor_scalar(w_hi[:, :, :], w_raw[:, :, :], 1.0, 1.0, ALU.mult, ALU.mult).then_inc(pool_self, 1)

            for r, slots in enumerate(LN_SLOTS):
                pool.sem_inc(ln[r]["lo"], slots)
            pool.wait_ge(pool_self, 1)
            with pool.Fori(0, NP // 2) as g:
                for slot in range(2):
                    ln_rstd(0, 0, g, slot)
            pool.wait_ge(wraw_s, 16)
            split_w()
            pool.wait_ge(pool_self, 2)
            g_.tensor_tensor(w_lo[:, :, :], w_raw[:, :, :], w_hi[:, :, :].bitcast(F32), ALU.subtract).then_inc(w_ready, 1)
            with pool.Fori(0, NP // 2) as g:
                for slot in range(2):
                    ln_low(0, 0, g, slot)
            pool.wait_ge(gate_ok, 1)
            with pool.Fori(0, B) as b:
                with pool.Fori(0, NKV) as g:
                    t = b * NKV + g
                    pool.wait_ge(wpraw_s, (t + 1) * 16)
                    g_.tensor_tensor(wp_raw[:, :, :], wp_raw[:, :, :],
                                     ga_row[:, bass.ds(b, 1), :].to_broadcast([P, QPG, HID]), ALU.mult).then_inc(pool_self, 1)
                    pool.wait_ge(y_done, this(y_done, t, 0))
                    pool.wait_ge(pool_self, t * 3 + 3)
                    pool.sem_inc(pool_gate, 1)
                    g_.tensor_scalar(wp_hi[:, :, :], wp_raw[:, :, :], 1.0, 1.0, ALU.mult, ALU.mult).then_inc(pool_self, 1)
                    pool.wait_ge(pool_self, t * 3 + 4)
                    g_.tensor_tensor(wp_lo[:, :, :], wp_raw[:, :, :], wp_hi[:, :, :].bitcast(F32), ALU.subtract).then_inc(wp_ready, 1)
                    ln_rstd(1, b, g, 0)
                    for s, i in enumerate(STEPS):
                        for h in range(QPG):
                            e = QPG * s + h
                            pool.wait_ge(rinv_done, this(rinv_done, t, e + 1))
                            pool.sem_inc(pool_gate, 1)
                            row = prob[:, s % 2, h, 0:(i + 1) * P]
                            g_.tensor_scalar(row, row, rinv[:, s % 2, h:h + 1], 1.0, ALU.mult, ALU.mult).then_inc(prob_done, 1)
                        if s == 0:
                            ln_low(1, b, g, 0)
                        if s == 1:
                            pool.wait_ge(wraw_s, (t + 2) * 16)
                            pool.wait_ge(qkv_done, this(qkv_done, t, 12))
                            pool.sem_inc(pool_gate, 1)
                            split_w()
                            pool.wait_ge(pool_self, t * 3 + 5)
                            g_.tensor_tensor(w_lo[:, :, :], w_raw[:, :, :], w_hi[:, :, :].bitcast(F32),
                                             ALU.subtract).then_inc(w_ready, 1)
            with pool.Fori(0, NP // 2) as g:
                for slot in range(2):
                    ln_rstd(2, 0, g, slot)
            with pool.Fori(0, NP // 2) as g:
                for slot in range(2):
                    ln_low(2, 0, g, slot)

            def raw_high(n):
                if n >= 2:
                    pool.wait_ge(fmm_s, (n - 1) * KH)
                g_.tensor_scalar(raw_hi[n % 2], raw[n], 1.0, 1.0, ALU.mult, ALU.mult).then_inc(rhi_s, 1)

            pool.wait_ge(raw_s[0], 16)
            pool.wait_ge(y_done, (TURNS + 1) * NT)
            raw_high(0)
            pool.wait_ge(raw_s[1], 16)
            raw_high(1)
            pool.wait_ge(raw_s[4], 16)
            a = raw_dn
            g_.tensor_tensor(sum_dn, a[:, :, :, 0, :], a[:, :, :, 1, :], ALU.add)
            g_.tensor_tensor(dif_dn, a[:, :, :, 0, :], a[:, :, :, 1, :], ALU.subtract).then_inc(fly_s, 1)
            pool.wait_ge(raw_s[2], 16)
            raw_high(2)
            pool.wait_ge(fly_s, 1)
            for one, z in enumerate((sum_dn, dif_dn)):
                g_.tensor_tensor(a[:, 0, :, one, :], z[:, 0, :, :], z[:, 1, :, :], ALU.add)
                last = g_.tensor_tensor(a[:, 1, :, one, :], z[:, 0, :, :], z[:, 1, :, :], ALU.subtract)
            last.then_inc(fly_s, 1)
            pool.wait_ge(raw_s[3], 16)
            raw_high(3)
            pool.wait_ge(fly_s, 2)
            raw_high(4)
            raw_high(5)

        @block.scalar
        def _(act):
            a_ = nc.scalar
            for s, n in PER_ACT.items():
                act.sem_inc(s, n)
            act.sem_inc(yt_s, KH)
            act.dma_start(sc[:, 0, :, :], c_cols).then_inc(small_s, 16)
            act.dma_start(ident[:, :], ident_in).then_inc(small_s, 16)
            act.dma_start(mask_f[:, 0, :], mask_in).then_inc(small_s, 16)
            act.dma_start(su_u[:, :], su_ug).then_inc(small_s, 16)
            act.dma_start(su_d[:, :], su_dp).then_inc(small_s, 16)
            act.dma_start(ws_u[:, :], ws_ug).then_inc(small_s, 16)
            act.dma_start(ws_d[:, :], ws_dp).then_inc(small_s, 16)
            act.wait_ge(small_s, 7 * 16)
            a_.activation(sc[:, 1, :, :], sc[:, 0, :, :], ACT.Exp, scale=-1.0).then_inc(silu_e, 1)

            for r, slots in enumerate(LN_SLOTS):
                act.sem_inc(ln[r]["hi"], slots)

            def ln_modulate(r, b, g, slot):
                n, block, batch, which = ln_step(r, b, g, slot)
                shift, gain = SA + 3 * which, CA + 3 * which
                at = bass.ds(block * P, LP * P)
                act.wait_ge(ln[r]["lo"], n + 1)
                act.wait_ge(ln[r]["tr"], n + LN_SLOTS[r] + 1)
                act.sem_inc(act_gate, 1)
                for k in range(KH):
                    for to in (h32[slot][:, k, :], h_hi[:, k, at]):
                        last = a_.activation(to, ln_bank[r][slot][:, k * LP * P:(k + 1) * LP * P], ACT.Identity,
                                             scale=cols[:, bass.ds(gain, 1), k, bass.ds(batch, 1)].rearrange("p a b -> p (a b)"),
                                             bias=cols[:, bass.ds(shift, 1), k, bass.ds(batch, 1)].rearrange("p a b -> p (a b)"))
                last.then_inc(ln[r]["hi"], 1)

            act.wait_ge(mod_ok, 1)
            with act.Fori(0, NP // 2) as g:
                for slot in range(2):
                    ln_modulate(0, 0, g, slot)
            with act.Fori(0, B) as b:
                with act.Fori(0, NKV) as g:
                    t = b * NKV + g

                    def v_high():
                        for n in range(2):
                            act.wait_ge(vtr_done, this(vtr_done, t, n + 1))
                            a_.activation(v_hi[:, 4 * n:4 * n + 4, :].rearrange("p j d -> p (j d)"), T[n],
                                          ACT.Copy).then_inc(v_hi_s, 1)

                    def chunk(c):
                        what, h, half = CHUNKS[c]
                        act.wait_ge(qkv_done, this(qkv_done, t, c + 1))
                        span = slice(half * CH, (half + 1) * CH)
                        if what == "v":
                            a_.activation(vt[:, span], bank(c), ACT.Copy).then_inc(vt_done, 1)
                        elif what == "k":
                            a_.activation(k_hi[:, span], bank(c), ACT.Copy).then_inc(qkv_hi, 1)
                        else:
                            a_.activation(q_hi[:, h, span], bank(c), ACT.Copy, scale=SCALE).then_inc(qkv_hi, 1)

                    waiting = []

                    def exps():
                        while waiting:
                            i, h = waiting.pop(0)
                            s = NT - 1 - i
                            nb, w = halves(i)
                            act.wait_ge(max_done, this(max_done, t, QPG * s + h + 1))
                            a_.activation(prob[:, s % 2, h, 0:nb * w].rearrange("p (a n) -> p a n", a=nb),
                                          S[h % 2][:, :].rearrange("p (a n) -> p a n", a=2)[:, 0:nb, 0:w],
                                          ACT.Exp, bias=nmax[:, s % 2, h:h + 1],
                                          accum_out=rsum[:, s % 2, h:h + 1]).then_inc(exp_done, 1)

                    for what, n, h in WALK:
                        if what == "C":
                            chunk(n)
                            if n == 6:
                                v_high()
                            exps()
                        if what == "L":
                            ln_modulate(1, b, g, 0)
                        if what == "S":
                            exps()
                            waiting.append((n, h))
                        if what == "T":
                            act.wait_ge(t_done, this(t_done, t, n + 1))
                            a_.activation(pt_hi[:, n % 3, :], T[n % 2], ACT.Copy).then_inc(pth_done, 1)
                            exps()
                        if what == "V" and n == LAST[UNITS[n][0]]:
                            s = NT - 1 - UNITS[n][0]
                            act.wait_ge(pv_done, this(pv_done, t, n + 1))
                            a_.activation(o_hi[:, s % 2, :], X[s % 2], ACT.Copy).then_inc(oh_done, 1)

            with act.Fori(0, NP // 2) as g:
                for slot in range(2):
                    ln_modulate(2, 0, g, slot)
            for n in range(6):
                for k in range(KH):
                    act.wait_ge(fmm_s, n * KH + k + 1)
                    if n < 4:
                        a_.activation(wu_hi[:, k, n * CH:(n + 1) * CH], bank(n % 2 * 2 + k), ACT.Identity,
                                      scale=su_u[:, k:k + 1]).then_inc(fhi_s, 1)
                    else:
                        for one in range(2):
                            m = 2 * (n - 4) + one
                            last = a_.activation(wd_hi[k][:, m, :], bank(n % 2 * 2 + k)[:, one * HID:(one + 1) * HID],
                                                 ACT.Identity, scale=su_d[:, 4 * k + m:4 * k + m + 1])
                        last.then_inc(fhi_s, 1)

            def gate(c, m):
                act.wait_ge(g32_s, c * NM + m + 1)
                act.wait_ge(gu_s, c * NM + m + 1)
                a_.activation(silu[:, m % 2, :], S[m % 2][:, 0:CH], ACT.Silu,
                              scale=ws_u[:, NM + m:NM + m + 1]).then_inc(silu_s, 1)

            def down_out(c):
                act.wait_ge(ytr_s, c * KH + KH)
                for k in range(KH):
                    act.wait_ge(dn_s, c * KH + k + 1)
                    act.sem_inc(act_gate, 1)
                    a_.activation(yt[:, k, :], X[k], ACT.Identity,
                                  scale=cols[:, GB, k, bass.ds(c // NC_B, 1)]).then_inc(yt_s, 1)

            for m in range(NM):
                gate(0, m)
            with act.Fori(1, B * NC_B) as c:
                gate(c, 0)
                down_out(c - 1)
                for m in range(1, NM):
                    gate(c, m)
            down_out(B * NC_B - 1)

        @block.vector
        def _(dve):
            v_ = nc.vector
            for s, n in PER_DVE.items():
                dve.sem_inc(s, n)
            dve.sem_inc(g32_s, 2)
            dve.sem_inc(fin_s, 2)
            count = [0]

            def link(ins):
                count[0] += 1
                ins.then_inc(dve_self, 1)
                dve.wait_ge(dve_self, count[0])

            dve.wait_ge(silu_e, 1)
            v_.tensor_copy(ident_b[:, :], ident[:, :])
            v_.tensor_copy(mask_b[:, :], mask_f[:, 0, :])
            link(v_.tensor_scalar(sc[:, 2, :, :], sc[:, 1, :, :], 1.0, None, ALU.add))
            link(v_.reciprocal(sc[:, 3, :, :], sc[:, 2, :, :]))
            link(v_.tensor_tensor(sc[:, 1, :, :], sc[:, 0, :, :], sc[:, 3, :, :], ALU.mult))
            v_.tensor_copy(scb[:, :, :, :], sc[:, 1, :, :].unsqueeze(3).to_broadcast([P, KH, B, P])).then_inc(silu_c, 1)

            def guard(dst, tmp1, tmp2):
                link(v_.scalar_tensor_tensor(tmp1, dst, -1.0, dst, ALU.mult, ALU.max))
                link(v_.tensor_scalar(tmp1, tmp1, 0.25, None, ALU.max))
                link(v_.tensor_scalar(tmp2, dst, 0.0, 2.0, ALU.is_ge, ALU.mult))
                return v_.scalar_tensor_tensor(dst, tmp2, -1.0, tmp1, ALU.add, ALU.mult)

            def ln_front(r, b, g, slot):
                s = ln[r]
                n, block, _, _ = ln_step(r, b, g, slot)
                for j in range(LP):
                    last = v_.bn_stats(stats[:, slot, j, :], x[:, bass.ds(block + j, 1), :].rearrange("p a n -> p (a n)"))
                last.then_inc(s["stats"], 1)
                dve.wait_ge(s["stats"], n + 1)
                dve.sem_inc(dve_gate, 1)
                for j in range(LP):
                    last = v_.bn_aggr(mv[:, slot, j, :], stats[:, slot, j, :])
                last.then_inc(s["aggr"], 1)
                dve.wait_ge(s["aggr"], n + 1)
                v_.tensor_scalar(vare[:, slot, :], mv[:, slot, :, 1], EPS, None, ALU.add).then_inc(s["vare"], 1)

            def ln_normalise(r, b, g, slot):
                s = ln[r]
                n, block, _, _ = ln_step(r, b, g, slot)
                dve.wait_ge(s["tr"], n + 1)
                dve.wait_ge(s["rstd"], n + 1)
                for j in range(LP):
                    last = v_.tensor_scalar(xhat[slot][:, j, :], x[:, bass.ds(block + j, 1), :].rearrange("p a n -> p (a n)"),
                                            mv[:, slot, j, 0:1], rstd[:, slot, j:j + 1], ALU.subtract, ALU.mult)
                last.then_inc(s["xhat"], 1)

            def ln_all(r):
                with dve.Fori(0, NP // 2) as g:
                    for slot in range(2):
                        ln_front(r, 0, g, slot)
                    for slot in range(2):
                        ln_normalise(r, 0, g, slot)

            dve.wait_ge(x_in_s[0], NC_B * 16)
            ln_all(0)
            dve.wait_ge(mod_mm, 1)
            link(v_.tensor_copy(cols[:, :, :, :], X[1][:, 0:24].rearrange("p (v k b) -> p v k b", v=6, k=KH)))
            for v in (CA, CB):
                last = v_.tensor_scalar(cols[:, v, :, :], cols[:, v, :, :], 1.0, None, ALU.add)
            last.then_inc(mod_ok, 1)
            link(v_.tensor_copy(ga_row[:, :, :], X[0].rearrange("p (b n) -> p b n", b=B)))
            guard(ga_row[:, :, :], guard_a, guard_b).then_inc(gate_ok, 1)
            link(guard(cols[:, GB, :, :], sc[:, 2, :, :], sc[:, 3, :, :]))
            link(v_.tensor_tensor(cols[:, GB, :, :], cols[:, GB, :, :],
                                  ws_d[:, :].unsqueeze(2).to_broadcast([P, KH, B]), ALU.mult))
            dve.wait_ge(x_in_s[1], NC_B * 16)

            with dve.Fori(0, B) as b:
                with dve.Fori(0, NKV) as g:
                    t = b * NKV + g

                    def chunk(c):
                        what, h, half = CHUNKS[c]
                        if what == "v":
                            return
                        span = slice(half * CH, (half + 1) * CH)
                        dve.wait_ge(qkv_hi, this(qkv_hi, t, c - 1))
                        if what == "k":
                            v_.tensor_tensor(k_lo[:, span], bank(c), k_hi[:, span].bitcast(F32), ALU.subtract).then_inc(qkv_lo, 1)
                        else:
                            v_.scalar_tensor_tensor(q_lo[:, h, span], bank(c), SCALE, q_hi[:, h, span].bitcast(F32),
                                                    ALU.mult, ALU.subtract).then_inc(qkv_lo, 1)

                    def v_low():
                        for n in range(2):
                            dve.wait_ge(v_hi_s, this(v_hi_s, t, n + 1))
                            v_.tensor_tensor(v_lo[:, 4 * n:4 * n + 4, :].rearrange("p j d -> p (j d)"), T[n],
                                             v_hi[:, 4 * n:4 * n + 4, :].rearrange("p j d -> p (j d)").bitcast(F32),
                                             ALU.subtract).then_inc(v_lo_s, 1)

                    waiting = []

                    def inverse():
                        while waiting:
                            i, h = waiting.pop(0)
                            s = NT - 1 - i
                            dve.wait_ge(exp_done, this(exp_done, t, QPG * s + h + 1))
                            v_.reciprocal(rinv[:, s % 2, h:h + 1], rsum[:, s % 2, h:h + 1]).then_inc(rinv_done, 1)

                    for what, n, h in WALK:
                        if what == "C":
                            chunk(n)
                            inverse()
                            if n == 6:
                                v_low()
                            if n == 7:
                                dve.wait_ge(add_done, this(add_done, t, 0))
                                ln_front(1, b, g, 0)
                            if n == 11:
                                ln_normalise(1, b, g, 0)
                        if what == "S":
                            s = NT - 1 - n
                            nb, w = halves(n)
                            dve.wait_ge(s_done, this(s_done, t, QPG * s + h + 1))
                            v_.tensor_reduce(nmax[:, s % 2, h:h + 1],
                                             S[h % 2][:, :].rearrange("p (a n) -> p a n", a=2)[:, 0:nb, 0:w],
                                             AX.XY, ALU.max, negate=True).then_inc(max_done, 1)
                            inverse()
                            waiting.append((n, h))
                        if what == "T":
                            dve.wait_ge(pth_done, this(pth_done, t, n + 1))
                            v_.tensor_tensor(pt_lo[:, n % 3, :], T[n % 2], pt_hi[:, n % 3, :].bitcast(F32),
                                             ALU.subtract).then_inc(ptl_done, 1)
                            inverse()
                        if what == "V" and n == LAST[UNITS[n][0]]:
                            s = NT - 1 - UNITS[n][0]
                            dve.wait_ge(oh_done, this(oh_done, t, s + 1))
                            v_.tensor_tensor(o_lo[:, s % 2, :], X[s % 2], o_hi[:, s % 2, :].bitcast(F32),
                                             ALU.subtract).then_inc(ol_done, 1)
                        if what == "Y":
                            s = NT - 1 - n
                            dve.wait_ge(y_done, this(y_done, t, s + 1))
                            row = x[:, bass.ds(b * NT + n, 1), :].rearrange("p a n -> p (a n)")
                            v_.tensor_tensor(row, X[s % 2][:, 0:HID], row, ALU.add).then_inc(add_done, 1)

            dve.wait_ge(t_done, (TURNS + 1) * NU)
            dve.wait_ge(add_done, (TURNS + 1) * NT)
            ln_all(2)
            dve.wait_ge(had_s, 16)
            dve.wait_ge(w_ready, TURNS + 1)
            for n in range(2):
                last = v_.tensor_copy(had_r[n], had_f[:, n, :])
            last.then_inc(had_ok, 1)

            def raw_low(n):
                dve.wait_ge(rhi_s, n + 1)
                v_.tensor_tensor(raw_lo[n % 2], raw[n], raw_hi[n % 2].bitcast(F32), ALU.subtract).then_inc(rlo_s, 1)

            raw_low(0)
            for n in range(6):
                if n < 5:
                    raw_low(n + 1)
                for k in range(KH):
                    dve.wait_ge(fhi_s, n * KH + k + 1)
                    src = bank(n % 2 * 2 + k)
                    if n < 4:
                        at = slice(n * CH, (n + 1) * CH)
                        v_.scalar_tensor_tensor(wu_lo[:, k, at], src, su_u[:, k:k + 1], wu_hi[:, k, at].bitcast(F32),
                                                ALU.mult, ALU.subtract).then_inc(wf_ok, 1)
                    else:
                        for one in range(2):
                            m = 2 * (n - 4) + one
                            last = v_.scalar_tensor_tensor(wd_lo[k][:, m, :], src[:, one * HID:(one + 1) * HID],
                                                           su_d[:, 4 * k + m:4 * k + m + 1], wd_hi[k][:, m, :].bitcast(F32),
                                                           ALU.mult, ALU.subtract)
                        last.then_inc(wf_ok, 1)

            def gated(c, m):
                dve.wait_ge(silu_s, c * NM + m + 1)
                v_.scalar_tensor_tensor(g32[:, m % 2, :], S[m % 2][:, CH:2 * CH], ws_u[:, m:m + 1], silu[:, m % 2, :],
                                        ALU.mult, ALU.mult).then_inc(g32_s, 1)
                dve.wait_ge(g32_s, c * NM + m + 3)
                v_.tensor_copy(g_hi[:, m % 2, :], g32[:, m % 2, :]).then_inc(ghi_s, 1)
                dve.wait_ge(ghi_s, c * NM + m + 1)
                v_.tensor_tensor(g_lo[:, m % 2, :], g32[:, m % 2, :], g_hi[:, m % 2, :].bitcast(F32),
                                 ALU.subtract).then_inc(g_ok, 1)

            def finish(c):
                dve.wait_ge(out_s, (c + 1) * 16)
                for a in range(2):
                    dve.wait_ge(ytr_s, (c + 1) * KH + a + 1)
                    v_.tensor_tensor(o_out[:, 2 * a:2 * a + 2, :], T[a].rearrange("p (j n) -> p j n", j=2),
                                     x[:, bass.ds(c * CT + 2 * a, 2), :], ALU.add).then_inc(fin_s, 1)

            for m in range(NM):
                gated(0, m)
            with dve.Fori(1, B * NC_B) as c:
                gated(c, 0)
                gated(c, 1)
                finish(c - 1)
                for m in range(2, NM):
                    gated(c, m)
            finish(B * NC_B - 1)

        @block.tensor
        def _(pe):
            mm, tr = nc.tensor.matmul, nc.tensor.transpose
            for s, n in PER_PE.items():
                pe.sem_inc(s, n)
            pe.sem_inc(ytr_s, KH)

            def three(dst, w_h, w_l, r_h, r_l, start, stop):
                mm(dst, w_h, r_h, start=start, stop=False)
                mm(dst, w_h, r_l, start=False, stop=False)
                return mm(dst, w_l, r_h, start=False, stop=stop)

            pe.wait_ge(silu_c, 1)
            pe.wait_ge(wmod_s, 16)
            for v in range(6):
                for k in range(KH):
                    for a in range(KH):
                        at = (v * KH + k) * B
                        mm(X[1][:, at:at + B], wmod_sb[:, a, v * HID + k * P:v * HID + (k + 1) * P], sc[:, 1, a, :],
                           start=a == 0, stop=a == KH - 1)
            for b in range(B):
                for a in range(KH):
                    last = mm(X[0][:, b * HID:(b + 1) * HID], scb[:, a, b, :], wmod_sb[:, a, GA * HID:(GA + 1) * HID],
                              start=a == 0, stop=a == KH - 1)
            last.then_inc(mod_mm, 1)

            for r, slots in enumerate(LN_SLOTS):
                pe.sem_inc(ln[r]["tr"], slots)

            def ln_transpose(r, b, g, slot):
                n = ln_step(r, b, g, slot)[0]
                if r != 1:
                    pe.wait_ge(ln[r]["hi"], n + 1)
                pe.wait_ge(ln[r]["xhat"], n + 1)
                for k in range(KH):
                    for j in range(LP):
                        last = tr(ln_bank[r][slot][:, (k * LP + j) * P:(k * LP + j + 1) * P],
                                  xhat[slot][:, j, k * P:(k + 1) * P], ident[:, :])
                last.then_inc(ln[r]["tr"], 1)

            with pe.Fori(0, NP // 2) as g:
                for slot in range(2):
                    ln_transpose(0, 0, g, slot)
            pe.wait_ge(ln[0]["lo"], NP + LN_SLOTS[0])
            pe.wait_ge(gate_ok, 1)
            with pe.Fori(0, B) as b:
                with pe.Fori(0, NKV) as g:
                    t = b * NKV + g

                    def chunk(c):
                        what, h, half = CHUNKS[c]
                        if c == 0:
                            pe.wait_ge(exp_done, this(exp_done, t, 0))
                            pe.wait_ge(w_ready, t + 1)
                            pe.wait_ge(ln[1]["lo"], t + 1)
                        elif c in (4, 5):
                            pe.wait_ge(vt_done, this(vt_done, t, c - 3))
                        elif c in (6, 7):
                            pe.wait_ge(qkv_lo, this(qkv_lo, t, c - 5))
                        elif c == 8:
                            pe.wait_ge(add_done, this(add_done, t, 0))
                        elif c >= 10:
                            pe.wait_ge(qkv_lo, this(qkv_lo, t, c - 3))
                        at = {"q": h, "k": QPG, "v": QPG + 1}[what] * D
                        span = bass.ds(b * SEQ + half * CH, CH)
                        for k in range(KH):
                            last = three(bank(c), w_hi[:, k, at:at + D], w_lo[:, k, at:at + D],
                                         h_hi[:, k, span], h_lo[:, k, span], k == 0, k == KH - 1)
                        last.then_inc(qkv_done, 1)

                    def v_transpose():
                        pe.wait_ge(ptl_done, this(ptl_done, t, 0))
                        for n in range(2):
                            pe.wait_ge(vt_done, this(vt_done, t, n + 1))
                            for j in range(4):
                                last = tr(T[n][:, j * P:(j + 1) * P], vt[:, (4 * n + j) * P:(4 * n + j + 1) * P], ident[:, :])
                            last.then_inc(vtr_done, 1)

                    for what, n, h in WALK:
                        if what == "C":
                            chunk(n)
                        if what == "VT":
                            v_transpose()
                        if what == "L":
                            pe.wait_ge(qkv_lo, this(qkv_lo, t, 10))
                            ln_transpose(1, b, g, 0)
                        if what == "S":
                            s = NT - 1 - n
                            e = QPG * s + h
                            if e < 2:
                                pe.wait_ge(qkv_lo, this(qkv_lo, t, 4 + 2 * e))
                            else:
                                pe.wait_ge(exp_done, this(exp_done, t, e - 1))
                            nb, w = halves(n)
                            wide = max(w, 2 * P)
                            q_at = slice(n * P, (n + 1) * P)
                            for a in range(nb):
                                mm(S[h % 2][:, a * CH:a * CH + wide], q_hi[:, h, q_at], k_hi[:, a * w:a * w + wide],
                                   start=True, stop=False)
                            at = (nb - 1) * CH + w - P
                            mm(S[h % 2][:, at:at + P], ident_b[:, :], mask_b[:, :], start=False, stop=False)
                            for a in range(nb):
                                mm(S[h % 2][:, a * CH:a * CH + wide], q_hi[:, h, q_at], k_lo[:, a * w:a * w + wide],
                                   start=False, stop=False)
                            for a in range(nb):
                                last = mm(S[h % 2][:, a * CH:a * CH + wide], q_lo[:, h, q_at], k_hi[:, a * w:a * w + wide],
                                          start=False, stop=True)
                            last.then_inc(s_done, 1)
                        if what == "T":
                            i, j = UNITS[n]
                            s = NT - 1 - i
                            if n >= 2:
                                pe.wait_ge(ptl_done, this(ptl_done, t, n - 1))
                            else:
                                pe.wait_ge(v_lo_s, this(v_lo_s, t, n + 1))
                            for h in range(QPG):
                                if j == 0:
                                    pe.wait_ge(prob_done, this(prob_done, t, QPG * s + h + 1))
                                last = tr(T[n % 2][:, h * P:(h + 1) * P], prob[:, s % 2, h, j * P:(j + 1) * P], ident[:, :])
                            last.then_inc(t_done, 1)
                        if what == "V":
                            i, j = UNITS[n]
                            s = NT - 1 - i
                            if j == 0 and s == 0:
                                pe.wait_ge(qkv_lo, this(qkv_lo, t, 9))
                            elif j == 0 and s == 1:
                                pe.wait_ge(ln[1]["hi"], t + 2)
                            elif j == 0:
                                pe.wait_ge(add_done, this(add_done, t, s - 1))
                            if n == 0:
                                pe.wait_ge(v_lo_s, this(v_lo_s, t, 2))
                            pe.wait_ge(ptl_done, this(ptl_done, t, n + 1))
                            three(X[s % 2], v_hi[:, j, :], v_lo[:, j, :], pt_hi[:, n % 3, :], pt_lo[:, n % 3, :],
                                  j == 0, j == i).then_inc(pv_done, 1)
                        if what == "Y":
                            s = NT - 1 - n
                            if s == 0:
                                pe.wait_ge(wp_ready, t + 2)
                            pe.wait_ge(ol_done, this(ol_done, t, s + 1))
                            for h in range(QPG):
                                last = three(X[s % 2][:, 0:HID], o_hi[:, s % 2, h * P:(h + 1) * P], o_lo[:, s % 2, h * P:(h + 1) * P],
                                             wp_hi[:, h, :], wp_lo[:, h, :], h == 0, h == QPG - 1)
                            last.then_inc(y_done, 1)

            with pe.Fori(0, NP // 2) as g:
                for slot in range(2):
                    ln_transpose(2, 0, g, slot)
            pe.wait_ge(had_ok, 1)
            for n in range(6):
                pe.wait_ge(rlo_s, n + 1)
                if n >= 2:
                    pe.wait_ge(wf_ok, KH * (n - 1))
                if n >= 4:
                    plus, minus = had_r[1][:, 0:P], had_r[1][:, P:2 * P]
                else:
                    plus, minus = had_r[0][:, 0:P], had_r[0][:, P:2 * P]
                for k in range(KH):
                    dst = bank(n % 2 * 2 + k)
                    for src in (0, 1):
                        mat = minus if k and src else plus
                        mm(dst, mat, raw_hi[n % 2][:, src, :], start=not src, stop=False)
                        last = mm(dst, mat, raw_lo[n % 2][:, src, :], start=False, stop=bool(src))
                    last.then_inc(fmm_s, 1)
            pe.wait_ge(wf_ok, 6 * KH)

            def gate_up(c, m):
                pe.wait_ge(g32_s, c * NM + m + 1)
                at = m // 2 * CH + m % 2 * P
                for a in (0, 1):
                    for k in range(KH):
                        col = at + (0 if a else 2 * P)
                        last = three(S[m % 2][:, a * CH:(a + 1) * CH], wu_hi[:, k, col:col + P], wu_lo[:, k, col:col + P],
                                     h_hi[:, k, bass.ds(c * CH, CH)], h_lo[:, k, bass.ds(c * CH, CH)],
                                     k == 0, k == KH - 1)
                last.then_inc(gu_s, 1)

            def down(c, m):
                if m == 0:
                    pe.wait_ge(yt_s, (c + 1) * KH)
                pe.wait_ge(g_ok, c * NM + m + 1)
                for k in range(KH):
                    last = three(X[k], wd_hi[m // 4][:, m % 4, k * P:(k + 1) * P], wd_lo[m // 4][:, m % 4, k * P:(k + 1) * P],
                                 g_hi[:, m % 2, :], g_lo[:, m % 2, :], m == 0, m == NM - 1)
                    if m == NM - 1:
                        last.then_inc(dn_s, 1)

            def back(c):
                pe.wait_ge(yt_s, (c + 2) * KH)
                for a in range(2):
                    pe.wait_ge(fin_s, c * 2 + a + 1)
                    for j in range(2):
                        for k in range(KH):
                            last = tr(T[a][:, j * HID + k * P:j * HID + (k + 1) * P],
                                      yt[:, k, (2 * a + j) * P:(2 * a + j + 1) * P], ident[:, :])
                    last.then_inc(ytr_s, 1)

            pe.wait_ge(ln[2]["hi"], NP + LN_SLOTS[2])
            pe.wait_ge(ln[1]["lo"], TURNS + LN_SLOTS[1])
            for m in range(NM):
                gate_up(0, m)
                if m:
                    down(0, m - 1)
            with pe.Fori(1, B * NC_B) as c:
                pe.wait_ge(ln[2]["lo"], NP + LN_SLOTS[2])
                gate_up(c, 0)
                down(c - 1, NM - 1)
                gate_up(c, 1)
                down(c, 0)
                back(c - 1)
                for m in range(2, NM):
                    gate_up(c, m)
                    down(c, m - 1)
            down(B * NC_B - 1, NM - 1)
            back(B * NC_B - 1)


def kernel(**inputs):
    import concourse.bacc as bacc
    from concourse.bass_utils import run_bass_kernel_spmd

    def get(name):
        return np.asarray(inputs[name])

    x = np.ascontiguousarray(get("L0_attn_x").reshape(B * NT, P, HID))
    w = get("L0_attn_weight_qkv").reshape(NKV, GW, KH, P).transpose(0, 3, 2, 1).reshape(NKV, P, KH * GW)
    w = np.concatenate([w, w[:1]])
    wp = get("L0_attn_weight_proj").reshape(HID, NKV, QPG, D).transpose(1, 3, 2, 0).reshape(NKV, P, QPG * HID)
    up_gate = np.stack([get("L0_ffn_W_up"), get("L0_ffn_W_gate")]).reshape(2, 4, 2 * P, KH, P)
    wug = up_gate.transpose(1, 4, 3, 0, 2).reshape(4, P, KH * CH)
    wdn = get("L0_ffn_W_down").reshape(HID, 2, 2, 2, P)
    wdn = wdn.transpose(4, 2, 1, 3, 0).reshape(P, NM * HID)
    n = np.arange(P)
    had = np.array([[1.0]])
    while len(had) < P:
        had = np.block([[had, had], [had, -had]])
    had = np.concatenate([s * had / n ** 0.5 for n in (HID, INTER) for s in (1, -1)], axis=1).astype(np.float32)
    arrays = {
        "x": x, "wqkv": w, "wproj": wp, "wmod": get("L0_wmod"),
        "c": get("L0_c").reshape(B, KH, P).transpose(2, 1, 0), "wug": wug, "wdn": wdn,
        "su_ug": get("L0_ffn_SU_ug").reshape(KH, P).T, "su_dp": get("L0_ffn_SU_dp").reshape(NM, P).T,
        "ws_ug": get("L0_ffn_Wscale_ug").reshape(2 * NM, P).T, "ws_dp": get("L0_ffn_Wscale_dp").reshape(KH, P).T,
        "ident": np.eye(P, dtype=np.float32),
        "mask": np.where(n[None, :] > n[:, None], MASKED, 0.0).astype(np.float32), "had": had,
    }
    nc = bacc.Bacc("TRN2", target_bir_lowering=False, num_devices=1)
    feed, args = {}, []
    for name, a in arrays.items():
        a = np.ascontiguousarray(a)
        feed[f"in_{name}"] = a
        args.append(nc.dram_tensor(f"in_{name}", a.shape, mybir.dt.from_np(a.dtype), kind="ExternalInput").ap())
    args.append(nc.dram_tensor("out_y", (B * NT, P, HID), F32, kind="ExternalOutput").ap())
    build(nc, *args)
    r = run_bass_kernel_spmd(nc, [feed], core_ids=[0])
    return r.results[0]["out_y"].reshape(B, SEQ, HID)
```

```python
import numpy as np
import concourse.bass as bass
from concourse import mybir
from contextlib import ExitStack

F32 = mybir.dt.float32
F32R = mybir.dt.float32r
ALU = mybir.AluOpType
ACT = mybir.ActivationFunctionType
AX = mybir.AxisListType

P = 128
B, SEQ, HID = 2, 1024, 256
NKV, QPG, D = 4, 4, 128
INTER = 1024
KH = HID // P
NT = SEQ // P
NM = INTER // P
CH = 512
CT = CH // P
NC_B = SEQ // CH
LP = 2
NP = NT // LP
GW = (QPG + 2) * D
SCALE = float(D) ** -0.5
EPS = 1e-5
MASKED = -1e30
STEPS = [NT - 1 - s for s in range(NT)]
UNITS = [(i, j) for i in STEPS for j in range(i + 1)]
NU = len(UNITS)
LAST = {i: max(n for n, u in enumerate(UNITS) if u[0] == i) for i in STEPS}
SA, CA, GA, SB, CB, GB = range(6)

SCORES_AT = {7: (0, 2, 4, 9), 6: (0, 1, 3, 6), 5: (0, 2, 3, 6), 4: (0, 1, 3, 4),
             3: (0, 0, 2, 3), 2: (0, 0, 0, 2), 1: (0, 0, 0, 2)}
PROJECT_AT = 1


def walk():
    out = [("C", 0, 0), ("C", 1, 0), ("C", 2, 0), ("C", 3, 0), ("VT", 0, 0), ("C", 4, 0), ("C", 5, 0), ("L", 0, 0)]
    for h in range(QPG):
        out += [("S", STEPS[0], h), ("C", 6 + h, 0)]
    out += [("C", 10, 0), ("S", STEPS[1], 0), ("C", 11, 0)]
    lag = 2

    def values(n):
        out.append(("V", n, 0))
        i, j = UNITS[n]
        if i < STEPS[0] and j == min(PROJECT_AT, i):
            out.append(("Y", i + 1, 0))

    for n, (i, j) in enumerate(UNITS[:-1]):
        out += [("S", i - 1, h) for h in range(QPG) if (n or h) and SCORES_AT[i][h] == 2 * j]
        out.append(("T", n, 0))
        out += [("S", i - 1, h) for h in range(QPG) if (n or h) and SCORES_AT[i][h] == 2 * j + 1]
        if n >= lag:
            values(n - lag)
    out += [("V", NU - 3, 0), ("V", NU - 2, 0), ("T", NU - 1, 0), ("Y", 2, 0), ("V", NU - 1, 0), ("Y", 1, 0), ("Y", 0, 0)]
    return out


WALK = walk()

PIECES = [0, 1, 4, 5, 2, 3]
FIRST = [("P", 0), ("P", 1), ("G", 0), ("P", 2), ("G", 1), ("D", 0), ("P", 3), ("G", 2), ("D", 1), ("P", 4), ("G", 3),
         ("D", 2), ("P", 5), ("G", 4), ("D", 3), ("L", 0), ("G", 5), ("D", 4), ("L", 1), ("G", 6), ("D", 5), ("L", 2),
         ("G", 7), ("L", 3), ("D", 6)]


def halves(i):
    n = (i + 1) * P
    return (2, n // 2) if n > CH else (1, n)


def build(nc, x_in, wqkv, wproj, wmod, c_cols, wug, wdn, su_ug, su_dp, ws_ug, ws_dp, ident_in, mask_in, had_in, out):
    ctx = ExitStack()
    with ctx:
        def sb(name, shape, dt=F32):
            return ctx.enter_context(nc.sbuf_tensor(name, shape, dt))

        def sem(name):
            return ctx.enter_context(nc.semaphore(name))

        x = sb("x", [P, B * NT, HID])
        h_hi = sb("h_hi", [P, KH, B * SEQ], F32R)
        h_lo = sb("h_lo", [P, KH, B * SEQ], F32R)
        q_hi = sb("q_hi", [P, QPG, SEQ], F32R)
        q_lo = sb("q_lo", [P, QPG, SEQ], F32R)
        k_hi = sb("k_hi", [P, SEQ], F32R)
        k_lo = sb("k_lo", [P, SEQ], F32R)
        v_hi = sb("v_hi", [P, NT, D], F32R)
        v_lo = sb("v_lo", [P, NT, D], F32R)
        prob = sb("prob", [P, 2, QPG, SEQ])
        pt_hi = sb("pt_hi", [P, 3, CH], F32R)
        pt_lo = sb("pt_lo", [P, 3, CH], F32R)
        o_hi = sb("o_hi", [P, 2, CH], F32R)
        o_lo = sb("o_lo", [P, 2, CH], F32R)
        w_raw = sb("w_raw", [P, KH, GW])
        w_hi = sb("w_hi", [P, KH, GW], F32R)
        w_lo = sb("w_lo", [P, KH, GW], F32R)
        wp_raw = sb("wp_raw", [P, QPG, HID])
        wp_hi = sb("wp_hi", [P, QPG, HID], F32R)
        wp_lo = sb("wp_lo", [P, QPG, HID], F32R)
        raw_down = sb("raw_down", [P, NM * HID])
        sum_dn, dif_dn = (sb(name, [P, 2, KH, HID])[:, :, :, :] for name in ("sum_down", "dif_down"))
        had_r = [sb(f"had_r{n}", [P, 2 * P], F32R)[:, :] for n in range(2)]
        ga_row = sb("ga_row", [P, B, HID])
        cols = sb("cols", [P, 6, KH, B])
        ident = sb("ident", [P, P])
        mask_f = sb("mask_f", [P, P])
        nmax = sb("nmax", [P, 2, QPG])
        rsum = sb("rsum", [P, 2, QPG])
        rinv = sb("rinv", [P, 2, QPG])
        xhat0 = sb("xhat", [P, LP, HID])
        h320 = sb("h32", [P, KH, LP * P])
        stats = sb("stats", [P, 2, LP, 6])
        mv = sb("mv", [P, 2, LP, 2])
        vare = sb("vare", [P, 2, LP])
        rstd = sb("rstd", [P, 2, LP])
        mhalf = sb("mhalf", [P, LP])
        mone = sb("mone", [P, 1])
        su_u = sb("su_u", [P, KH])
        su_d = sb("su_d", [P, NM])
        ws_u = sb("ws_u", [P, 2 * NM])
        ws_d = sb("ws_d", [P, KH])
        sc = sb("sc", [P, 4, KH, B])
        scb = sb("scb", [P, KH, B, P])

        flat = prob[:, :, :, :].rearrange("p a h n -> p (a h n)")

        def part(start, *shape):
            size = int(np.prod(shape))
            names = "abcd"[:len(shape)]
            return flat[:, start:start + size].rearrange(
                f"p ({' '.join(names)}) -> p {' '.join(names)}", **dict(zip(names, shape)))

        vt = prob[:, 1, 0, :]
        xhat = [xhat0, part(0, LP, HID)]
        h32 = [h320, part(512, KH, LP * P)]
        wmod_sb = part(1024, KH, 6 * HID)
        guard_a, guard_b = part(5248, B, HID), part(5760, B, HID)
        had_f = part(6272, 2, 2 * P)
        raw = [prob[:, n // 2, n % 2 * 2:n % 2 * 2 + 2, CH:2 * CH] for n in range(4)]
        raw += [raw_down[:, n * KH * CH:(n + 1) * KH * CH].rearrange("p (k n) -> p k n", k=KH) for n in range(2)]
        raw_dn = raw_down[:, :].rearrange("p (a k o n) -> p a k o n", a=2, k=KH, o=2)
        g32, silu, yt = (prob[:, n // 2, n % 2 * 2:n % 2 * 2 + 2, 0:CH] for n in range(3))
        o_out = prob[:, 1, 2, :].rearrange("p (t n) -> p t n", t=CT)
        raw_hi = [w_hi[:, :, 0:CH], o_hi[:, :, :]]
        raw_lo = [w_lo[:, :, 0:CH], o_lo[:, :, :]]
        wu_hi = q_hi[:, :, :].rearrange("p (k b) n -> p k (b n)", k=KH)
        wu_lo = q_lo[:, :, :].rearrange("p (k b) n -> p k (b n)", k=KH)
        wd_hi = [a[:, :].rearrange("p (m n) -> p m n", m=4) for a in (k_hi, k_lo)]
        wd_lo = [a[:, :, :].rearrange("p m d -> p (m d)").rearrange("p (m n) -> p m n", m=4) for a in (v_hi, v_lo)]
        g_hi, g_lo = pt_hi, pt_lo

        psum = [ctx.enter_context(nc.psum_tensor(f"ps{n}", [P, 2 * CH], F32)) for n in range(4)]
        S = [psum[0], psum[1]]
        T = [psum[2][:, 0:CH], psum[2][:, CH:2 * CH]]
        X = [psum[3][:, 0:CH], psum[3][:, CH:2 * CH]]
        O = [X[s % 2] for s in range(NT - 1)] + [psum[1][:, CH:2 * CH]]

        x_in_s = [sem(f"x_loaded{c}") for c in range(NC_B)] + [sem("x_loaded_rest")]
        c_s, ident_s, small_s = sem("c_loaded"), sem("ident_loaded"), sem("small_loaded")
        wmod_s = [sem(f"wmod_loaded{n}") for n in range(2)]
        wraw_s = sem("w_raw_loaded")
        wpraw_s = sem("wp_raw_loaded")
        consts = sem("constants_made")
        silu_e = sem("mod_exp")
        silu_c = sem("mod_silu")
        mod_mm = sem("mod_multiplied")
        mod_ok, gate_ok = sem("mod_ready"), sem("gate_ready")
        dve_self = sem("dve_self")
        pool_self = sem("pool_self")
        dve_gate, act_gate, pool_gate = sem("dve_gate"), sem("act_gate"), sem("pool_gate")
        ln = [{k: sem(f"ln{r}_{k}") for k in ("stats", "aggr", "vare", "rstd", "xhat", "tr", "h32", "hi", "lo")} for r in range(3)]
        LN_SLOTS = [2, 1, 1]
        qkv_done, qkv_hi, qkv_lo = sem("qkv_done"), sem("qkv_hi"), sem("qkv_lo")
        vt_done, vtr_done, v_hi_s, v_lo_s = sem("vt_done"), sem("vtr_done"), sem("v_hi_done"), sem("v_lo_done")
        s_done, masked, max_done, exp_done = sem("scores_done"), sem("masked"), sem("max_done"), sem("exp_done")
        rinv_done, prob_done = sem("rinv_done"), sem("prob_done")
        t_done, pth_done, ptl_done = sem("transposed"), sem("pt_hi_done"), sem("pt_lo_done")
        pv_done, oh_done, ol_done = sem("pv_done"), sem("o_hi_done"), sem("o_lo_done")
        y_done, add_done = sem("y_done"), sem("x_added")
        w_ready, wp_ready = sem("w_ready"), sem("wp_ready")
        raw_s = [sem(f"raw_loaded{n}") for n in range(5)]
        had_s, fly_s = sem("had_loaded"), sem("butterflies")
        rhi_s, rlo_s, fmm_s, fhi_s, wf_ok = (sem("raw_hi_done"), sem("raw_lo_done"), sem("hadamard_done"),
                                             sem("wf_hi"), sem("wf_ready"))
        rlo0_s, rhi1_s = sem("raw_lo_first_done"), sem("raw_hi_second_done")
        gu_s, silu_s, g32_s, ghi_s, g_ok = sem("gate_up_done"), sem("silu_done"), sem("g32_done"), sem("g_hi_done"), sem("g_ready")
        dn_s, yt_s, ytr_s, fin_s, out_s = sem("down_done"), sem("yt_done"), sem("y_transposed"), sem("out_ready"), sem("out_stored")

        PER_PE = {qkv_done: 12, vtr_done: 2, s_done: 32, t_done: NU, pv_done: NU, y_done: NT}
        PER_ACT = {qkv_hi: 10, vt_done: 2, v_hi_s: 2, exp_done: 32, pth_done: NU, oh_done: NT}
        PER_DVE = {qkv_lo: 10, v_lo_s: 2, masked: 32, max_done: 32, ptl_done: NU, ol_done: NT, add_done: NT}
        PER_POOL = {prob_done: 32, rinv_done: 32}
        per = {s.name: n for d in (PER_PE, PER_ACT, PER_DVE, PER_POOL) for s, n in d.items()}
        TURNS = B * NKV

        def this(s, t, k):
            return (t + 1) * per[s.name] + k

        CHUNKS = [("v", 0, 0), ("v", 0, 1), ("k", 0, 0), ("k", 0, 1)]
        CHUNKS += [("q", h, 1) for h in range(QPG)] + [("q", h, 0) for h in range(QPG)]

        def bank(c):
            return psum[c // 2][:, c % 2 * CH:(c % 2 + 1) * CH] if c < 4 else X[c % 2]

        def score_banks(i, h):
            at = 0 if halves(i)[0] == 2 else h // 2 * CH
            return S[h % 2][:, at:at + halves(i)[0] * CH]

        def ln_step(r, b, g, slot):
            if r == 1:
                return b * NKV + g, b * -NT + g * LP + NT, b * -1 + 1, b
            n = g * LN_SLOTS[r] + slot
            return n, r // 2 * NT + n * LP, r // 2, r // 2

        W = [X if n == 1 else T for n in range(len(PIECES))]

        def ln_bank(r, g, slot):
            return T[g % 2] if r == 2 else T[slot]


        block = ctx.enter_context(nc.Block())

        @block.sync
        def _(sp):
            sp.sem_inc(out_s, 16)
            def load_x(c):
                sp.dma_start(x[:, c * CT:(c + 1) * CT, :],
                             x_in[c * CT:(c + 1) * CT, :, :].rearrange("t p n -> p t n")).then_inc(x_in_s[min(c, NC_B)], 16)

            def load_wmod(n):
                part_n = slice((0, 2, 6)[n] * HID, (0, 2, 6)[n + 1] * HID)
                sp.dma_start(wmod_sb[:, :, part_n], wmod[:, part_n].rearrange("(k p) n -> p k n", p=P)).then_inc(wmod_s[n], 16)

            sp.dma_start(sc[:, 0, :, :], c_cols).then_inc(c_s, 16)
            load_x(0)
            load_wmod(0)
            load_x(1)
            load_wmod(1)
            sp.dma_start(w_raw[:, :, :], wqkv[0, :, :].rearrange("p (k n) -> p k n", k=KH)).then_inc(wraw_s, 16)
            load_x(2)
            load_x(3)
            sp.dma_start(had_f, had_in.rearrange("p (a n) -> p a n", a=2)).then_inc(had_s, 16)
            sp.dma_start(raw_down[:, :], wdn).then_inc(raw_s[4], 16)
            with sp.Fori(0, B) as b:
                with sp.Fori(0, NKV) as g:
                    t = b * NKV + g
                    sp.wait_ge(wp_ready, t + 1)
                    sp.dma_start(wp_raw[:, :, :],
                                 wproj[bass.ds(g, 1), :, :].rearrange("a p (h n) -> p (a h) n", h=QPG)).then_inc(wpraw_s, 16)
                    sp.wait_ge(w_ready, t + 1)
                    sp.dma_start(w_raw[:, :, :],
                                 wqkv[bass.ds(g + 1, 1), :, :].rearrange("a p (k n) -> p (a k) n", k=KH)).then_inc(wraw_s, 16)
            wide = sum(i + 1 for i in STEPS if i >= CT)
            sp.wait_ge(t_done, this(t_done, TURNS - 1, wide))
            for n in range(4):
                sp.dma_start(raw[n], wug[n, :, :].rearrange("p (k n) -> p k n", k=KH)).then_inc(raw_s[n], 16)
            with sp.Fori(0, B * NC_B) as c:
                sp.wait_ge(fin_s, (c + 2) * 2)
                sp.dma_start(out[bass.ds(c * CT, CT), :, :].rearrange("t p n -> p t n"), o_out).then_inc(out_s, 16)
            sp.wait_ge(out_s, 16 * (B * NC_B + 1))

        @block.gpsimd
        def _(pool):
            g_ = nc.gpsimd
            for s, n in PER_POOL.items():
                pool.sem_inc(s, n)
            pool.sem_inc(wp_ready, 1)
            g_.memset(mone[:, :], -1.0)
            g_.memset(mhalf[:, :], -0.5).then_inc(pool_self, 1)

            def ln_rstd(r, b, g, slot):
                n = ln_step(r, b, g, slot)[0]
                pool.wait_ge(ln[r]["vare"], n + 1)
                g_.tensor_tensor(rstd[:, slot, :], vare[:, slot, :], mhalf[:, :], ALU.pow).then_inc(ln[r]["rstd"], 1)

            def ln_low(r, b, g, slot):
                n, block, _, _ = ln_step(r, b, g, slot)
                pool.wait_ge(ln[r]["hi"], n + LN_SLOTS[r] + 1)
                at = bass.ds(block * P, LP * P)
                g_.tensor_tensor(h_lo[:, :, at], h32[slot][:, :, :], h_hi[:, :, at].bitcast(F32), ALU.subtract).then_inc(ln[r]["lo"], 1)

            def split_w():
                g_.tensor_scalar(w_hi[:, :, :], w_raw[:, :, :], 1.0, 1.0, ALU.mult, ALU.mult).then_inc(pool_self, 1)

            for r, slots in enumerate(LN_SLOTS):
                pool.sem_inc(ln[r]["lo"], slots)
            pool.wait_ge(pool_self, 1)
            for slot in range(2):
                ln_rstd(0, 0, 0, slot)
            for slot in range(2):
                ln_rstd(0, 0, 1, slot)
            pool.wait_ge(wraw_s, 16)
            split_w()
            for g in range(NP // 2):
                for slot in range(2):
                    ln_low(0, 0, g, slot)
            pool.wait_ge(raw_s[4], 16)
            a = raw_dn
            g_.tensor_tensor(sum_dn, a[:, :, :, 0, :], a[:, :, :, 1, :], ALU.add)
            g_.tensor_tensor(dif_dn, a[:, :, :, 0, :], a[:, :, :, 1, :], ALU.subtract).then_inc(fly_s, 1)
            pool.wait_ge(gate_ok, 1)
            with pool.Fori(0, B) as b:
                with pool.Fori(0, NKV) as g:
                    t = b * NKV + g
                    ln_rstd(1, b, g, 0)
                    pool.wait_ge(wpraw_s, (t + 1) * 16)
                    g_.tensor_tensor(wp_raw[:, :, :], wp_raw[:, :, :],
                                     ga_row[:, bass.ds(b, 1), :].to_broadcast([P, QPG, HID]), ALU.mult).then_inc(pool_self, 1)
                    pool.wait_ge(y_done, this(y_done, t, 0))
                    pool.wait_ge(pool_self, t * 3 + 3)
                    pool.sem_inc(pool_gate, 1)
                    g_.tensor_scalar(wp_hi[:, :, :], wp_raw[:, :, :], 1.0, 1.0, ALU.mult, ALU.mult).then_inc(pool_self, 1)
                    pool.wait_ge(pool_self, t * 3 + 4)
                    g_.tensor_tensor(wp_lo[:, :, :], wp_raw[:, :, :], wp_hi[:, :, :].bitcast(F32), ALU.subtract).then_inc(wp_ready, 1)
                    ln_low(1, b, g, 0)
                    for s, i in enumerate(STEPS):
                        for h in range(QPG):
                            e = QPG * s + h
                            pool.wait_ge(exp_done, this(exp_done, t, e + 1))
                            g_.tensor_tensor(rinv[:, s % 2, h:h + 1], rsum[:, s % 2, h:h + 1], mone[:, :],
                                             ALU.pow).then_inc(rinv_done, 1)
                            pool.wait_ge(rinv_done, this(rinv_done, t, e + 1))
                            pool.sem_inc(pool_gate, 1)
                            row = prob[:, s % 2, h, 0:(i + 1) * P]
                            g_.tensor_scalar(row, row, rinv[:, s % 2, h:h + 1], 1.0, ALU.mult, ALU.mult).then_inc(prob_done, 1)
                        if s == 1:
                            pool.wait_ge(wraw_s, (t + 2) * 16)
                            pool.wait_ge(qkv_done, this(qkv_done, t, 12))
                            pool.sem_inc(pool_gate, 1)
                            split_w()
                            pool.wait_ge(pool_self, t * 3 + 5)
                            g_.tensor_tensor(w_lo[:, :, :], w_raw[:, :, :], w_hi[:, :, :].bitcast(F32),
                                             ALU.subtract).then_inc(w_ready, 1)
            def raw_high(n):
                if n >= 2:
                    pool.wait_ge(fmm_s, (n - 1) * KH)
                g_.tensor_scalar(raw_hi[n % 2], raw[PIECES[n]], 1.0, 1.0, ALU.mult, ALU.mult).then_inc(rhi_s, 1)

            pool.wait_ge(raw_s[0], 16)
            raw_high(0)
            pool.wait_ge(rhi_s, 1)
            g_.tensor_tensor(raw_lo[0], raw[0], raw_hi[0].bitcast(F32), ALU.subtract).then_inc(rlo0_s, 1)
            pool.wait_ge(fly_s, 1)
            for one, z in enumerate((sum_dn, dif_dn)):
                g_.tensor_tensor(a[:, 0, :, one, :], z[:, 0, :, :], z[:, 1, :, :], ALU.add)
                last = g_.tensor_tensor(a[:, 1, :, one, :], z[:, 0, :, :], z[:, 1, :, :], ALU.subtract)
            last.then_inc(fly_s, 1)
            pool.wait_ge(fly_s, 2)
            for n in range(2, len(PIECES)):
                if PIECES[n] < 4:
                    pool.wait_ge(raw_s[PIECES[n]], 16)
                raw_high(n)
            ln_rstd(2, 0, 0, 0)
            for n in range(NP):
                if n + 1 < NP:
                    ln_rstd(2, 0, n + 1, 0)
                ln_low(2, 0, n, 0)

        @block.scalar
        def _(act):
            a_ = nc.scalar
            for s, n in PER_ACT.items():
                act.sem_inc(s, n)
            act.sem_inc(yt_s, KH)
            for r, slots in enumerate(LN_SLOTS):
                act.sem_inc(ln[r]["h32"], slots)
                act.sem_inc(ln[r]["hi"], slots)
            act.dma_start(ident[:, :], ident_in).then_inc(ident_s, 16)
            act.wait_ge(c_s, 16)
            a_.activation(sc[:, 1, :, :], sc[:, 0, :, :], ACT.Exp, scale=-1.0).then_inc(silu_e, 1)
            act.dma_start(mask_f[:, :], mask_in).then_inc(small_s, 16)
            act.dma_start(su_u[:, :], su_ug).then_inc(small_s, 16)
            act.dma_start(su_d[:, :], su_dp).then_inc(small_s, 16)
            act.dma_start(ws_u[:, :], ws_ug).then_inc(small_s, 16)
            act.dma_start(ws_d[:, :], ws_dp).then_inc(small_s, 16)

            def ln_modulate(r, b, g, slot):
                n, block, batch, which = ln_step(r, b, g, slot)
                shift, gain = SA + 3 * which, CA + 3 * which
                at = bass.ds(block * P, LP * P)
                act.wait_ge(ln[r]["lo"], n + 1)
                act.wait_ge(ln[r]["tr"], n + LN_SLOTS[r] + 1)
                if r == 1:
                    act.sem_inc(act_gate, 1)
                for k in range(KH):
                    for to in (h32[slot][:, k, :], h_hi[:, k, at])[:2 if r == 1 else 1]:
                        last = a_.activation(to, ln_bank(r, g, slot)[:, k * LP * P:(k + 1) * LP * P], ACT.Identity,
                                             scale=cols[:, bass.ds(gain, 1), k, bass.ds(batch, 1)].rearrange("p a b -> p (a b)"),
                                             bias=cols[:, bass.ds(shift, 1), k, bass.ds(batch, 1)].rearrange("p a b -> p (a b)"))
                last.then_inc(ln[r]["hi" if r == 1 else "h32"], 1)

            act.wait_ge(mod_ok, 1)
            for g in range(NP // 2):
                for slot in range(2):
                    ln_modulate(0, 0, g, slot)
            act.wait_ge(small_s, 5 * 16)
            with act.Fori(0, B) as b:
                with act.Fori(0, NKV) as g:
                    t = b * NKV + g

                    def v_high():
                        for n in range(2):
                            act.wait_ge(vtr_done, this(vtr_done, t, n + 1))
                            a_.activation(v_hi[:, 4 * n:4 * n + 4, :].rearrange("p j d -> p (j d)"), T[n],
                                          ACT.Copy).then_inc(v_hi_s, 1)

                    def chunk(c):
                        what, h, half = CHUNKS[c]
                        act.wait_ge(qkv_done, this(qkv_done, t, c + 1))
                        span = slice(half * CH, (half + 1) * CH)
                        if what == "v":
                            a_.activation(vt[:, span], bank(c), ACT.Copy).then_inc(vt_done, 1)
                        elif what == "k":
                            a_.activation(k_hi[:, span], bank(c), ACT.Copy).then_inc(qkv_hi, 1)
                        else:
                            a_.activation(q_hi[:, h, span], bank(c), ACT.Copy, scale=SCALE).then_inc(qkv_hi, 1)

                    waiting = []

                    def exps():
                        while waiting:
                            i, h = waiting.pop(0)
                            s = NT - 1 - i
                            nb, w = halves(i)
                            act.wait_ge(max_done, this(max_done, t, QPG * s + h + 1))
                            a_.activation(prob[:, s % 2, h, 0:nb * w].rearrange("p (a n) -> p a n", a=nb),
                                          score_banks(i, h).rearrange("p (a n) -> p a n", a=nb)[:, :, 0:w],
                                          ACT.Exp, bias=nmax[:, s % 2, h:h + 1],
                                          accum_out=rsum[:, s % 2, h:h + 1]).then_inc(exp_done, 1)

                    for what, n, h in WALK:
                        if what == "C":
                            chunk(n)
                            if n == 3:
                                v_high()
                            exps()
                        if what == "L":
                            ln_modulate(1, b, g, 0)
                        if what == "S":
                            exps()
                            waiting.append((n, h))
                        if what == "T":
                            act.wait_ge(t_done, this(t_done, t, n + 1))
                            a_.activation(pt_hi[:, n % 3, :], T[n % 2], ACT.Copy).then_inc(pth_done, 1)
                            exps()
                        if what == "V" and n == LAST[UNITS[n][0]]:
                            s = NT - 1 - UNITS[n][0]
                            act.wait_ge(pv_done, this(pv_done, t, n + 1))
                            a_.activation(o_hi[:, s % 2, :], O[s], ACT.Copy).then_inc(oh_done, 1)

            a_.activation(sc[:, 1, :, :], sc[:, 0, :, :], ACT.Silu)
            act.wait_ge(raw_s[1], 16)
            act.wait_ge(y_done, (TURNS + 1) * NT)
            a_.activation(raw_hi[1], raw[1], ACT.Copy).then_inc(rhi1_s, 1)

            def weights_high(n):
                piece = PIECES[n]
                for k in range(KH):
                    act.wait_ge(fmm_s, n * KH + k + 1)
                    if piece < 4:
                        a_.activation(wu_hi[:, k, piece * CH:(piece + 1) * CH], W[n][k], ACT.Identity,
                                      scale=su_u[:, k:k + 1]).then_inc(fhi_s, 1)
                    else:
                        for one in range(2):
                            m = 2 * (piece - 4) + one
                            last = a_.activation(wd_hi[k][:, m, :], W[n][k][:, one * HID:(one + 1) * HID],
                                                 ACT.Identity, scale=su_d[:, 4 * k + m:4 * k + m + 1])
                        last.then_inc(fhi_s, 1)

            def gate(c, m):
                act.wait_ge(g32_s, c * NM + m + 1)
                act.wait_ge(gu_s, c * NM + m + 1)
                a_.activation(silu[:, m % 2, :], S[m % 2][:, 0:CH], ACT.Silu,
                              scale=ws_u[:, NM + m:NM + m + 1]).then_inc(silu_s, 1)

            def down_out(c):
                act.wait_ge(ytr_s, c * KH + KH)
                for k in range(KH):
                    act.wait_ge(dn_s, c * KH + k + 1)
                    act.sem_inc(act_gate, 1)
                    a_.activation(yt[:, k, :], X[k], ACT.Identity,
                                  scale=cols[:, GB, k, bass.ds(c // NC_B, 1)]).then_inc(yt_s, 1)

            for what, n in FIRST:
                if what == "P":
                    weights_high(n)
                if what == "G":
                    gate(0, n)
                if what == "L":
                    ln_modulate(2, 0, n, 0)
            with act.Fori(1, B * NC_B) as c:
                gate(c, 0)
                down_out(c - 1)
                for m in range(1, NM):
                    gate(c, m)
            down_out(B * NC_B - 1)

        @block.vector
        def _(dve):
            v_ = nc.vector
            for s, n in PER_DVE.items():
                dve.sem_inc(s, n)
            dve.sem_inc(g32_s, 2)
            dve.sem_inc(fin_s, 2)
            count = [0]

            def link(ins):
                count[0] += 1
                ins.then_inc(dve_self, 1)
                dve.wait_ge(dve_self, count[0])

            dve.wait_ge(silu_e, 1)
            link(v_.tensor_scalar(sc[:, 2, :, :], sc[:, 1, :, :], 1.0, None, ALU.add))
            link(v_.reciprocal(sc[:, 3, :, :], sc[:, 2, :, :]))
            link(v_.tensor_tensor(sc[:, 1, :, :], sc[:, 0, :, :], sc[:, 3, :, :], ALU.mult))
            v_.tensor_copy(scb[:, :, :, :], sc[:, 1, :, :].unsqueeze(3).to_broadcast([P, KH, B, P])).then_inc(silu_c, 1)

            def guard(dst, tmp1, tmp2):
                link(v_.scalar_tensor_tensor(tmp1, dst, -1.0, dst, ALU.mult, ALU.max))
                link(v_.tensor_scalar(tmp1, tmp1, 0.25, None, ALU.max))
                link(v_.tensor_scalar(tmp2, dst, 0.0, 2.0, ALU.is_ge, ALU.mult))
                return v_.scalar_tensor_tensor(dst, tmp2, -1.0, tmp1, ALU.add, ALU.mult)

            def ln_front(r, b, g, slot):
                s = ln[r]
                n, block, _, _ = ln_step(r, b, g, slot)
                for j in range(LP):
                    last = v_.bn_stats(stats[:, slot, j, :], x[:, bass.ds(block + j, 1), :].rearrange("p a n -> p (a n)"))
                last.then_inc(s["stats"], 1)
                dve.wait_ge(s["stats"], n + 1)
                dve.sem_inc(dve_gate, 1)
                for j in range(LP):
                    last = v_.bn_aggr(mv[:, slot, j, :], stats[:, slot, j, :])
                last.then_inc(s["aggr"], 1)
                dve.wait_ge(s["aggr"], n + 1)
                v_.tensor_scalar(vare[:, slot, :], mv[:, slot, :, 1], EPS, None, ALU.add).then_inc(s["vare"], 1)

            def ln_normalise(r, b, g, slot):
                s = ln[r]
                n, block, _, _ = ln_step(r, b, g, slot)
                dve.wait_ge(s["tr"], n + 1)
                dve.wait_ge(s["rstd"], n + 1)
                for j in range(LP):
                    last = v_.tensor_scalar(xhat[slot][:, j, :], x[:, bass.ds(block + j, 1), :].rearrange("p a n -> p (a n)"),
                                            mv[:, slot, j, 0:1], rstd[:, slot, j:j + 1], ALU.subtract, ALU.mult)
                last.then_inc(s["xhat"], 1)

            def ln_high(r, b, g, slot):
                n, block, _, _ = ln_step(r, b, g, slot)
                dve.wait_ge(ln[r]["h32"], n + LN_SLOTS[r] + 1)
                v_.tensor_copy(h_hi[:, :, block * P:(block + LP) * P], h32[slot][:, :, :]).then_inc(ln[r]["hi"], 1)

            dve.wait_ge(x_in_s[0], 16)
            for slot in range(2):
                ln_front(0, 0, 0, slot)
            for slot in range(2):
                ln_normalise(0, 0, 0, slot)
            dve.wait_ge(x_in_s[1], 16)
            for slot in range(2):
                ln_front(0, 0, 1, slot)
            dve.wait_ge(mod_mm, 1)
            link(v_.tensor_copy(cols[:, 0:2, :, :], S[0][:, 0:2 * KH * B].rearrange("p (v k b) -> p v k b", v=2, k=KH)))
            v_.tensor_scalar(cols[:, CA, :, :], cols[:, CA, :, :], 1.0, None, ALU.add).then_inc(mod_ok, 1)
            for slot in range(2):
                ln_high(0, 0, 0, slot)
            for slot in range(2):
                ln_normalise(0, 0, 1, slot)
            dve.wait_ge(pool_self, 2)
            v_.tensor_tensor(w_lo[:, :, :], w_raw[:, :, :], w_hi[:, :, :].bitcast(F32), ALU.subtract).then_inc(w_ready, 1)
            for slot in range(2):
                ln_high(0, 0, 1, slot)
            dve.wait_ge(mod_mm, 2)
            v_.tensor_copy(ga_row[:, :, :], X[0].rearrange("p (b n) -> p b n", b=B))
            link(v_.tensor_copy(cols[:, SB:GB + 1, :, :], X[1][:, SB * KH * B:(GB + 1) * KH * B].rearrange("p (v k b) -> p v k b", v=3, k=KH)))
            dve.wait_ge(had_s, 16)
            for n in range(2):
                last = v_.tensor_copy(had_r[n], had_f[:, n, :])
            last.then_inc(consts, 1)
            dve.wait_ge(small_s, 5 * 16)
            v_.tensor_scalar(cols[:, CB, :, :], cols[:, CB, :, :], 1.0, None, ALU.add).then_inc(mod_ok, 1)
            guard(ga_row[:, :, :], guard_a, guard_b).then_inc(gate_ok, 1)
            link(guard(cols[:, GB, :, :], sc[:, 2, :, :], sc[:, 3, :, :]))
            link(v_.tensor_tensor(cols[:, GB, :, :], cols[:, GB, :, :],
                                  ws_d[:, :].unsqueeze(2).to_broadcast([P, KH, B]), ALU.mult))
            dve.wait_ge(x_in_s[2], (B - 1) * NC_B * 16)

            with dve.Fori(0, B) as b:
                with dve.Fori(0, NKV) as g:
                    t = b * NKV + g

                    def chunk(c):
                        what, h, half = CHUNKS[c]
                        if what == "v":
                            return
                        span = slice(half * CH, (half + 1) * CH)
                        dve.wait_ge(qkv_hi, this(qkv_hi, t, c - 1))
                        if what == "k":
                            v_.tensor_tensor(k_lo[:, span], bank(c), k_hi[:, span].bitcast(F32), ALU.subtract).then_inc(qkv_lo, 1)
                        else:
                            v_.scalar_tensor_tensor(q_lo[:, h, span], bank(c), SCALE, q_hi[:, h, span].bitcast(F32),
                                                    ALU.mult, ALU.subtract).then_inc(qkv_lo, 1)

                    def v_low():
                        for n in range(2):
                            dve.wait_ge(v_hi_s, this(v_hi_s, t, n + 1))
                            v_.tensor_tensor(v_lo[:, 4 * n:4 * n + 4, :].rearrange("p j d -> p (j d)"), T[n],
                                             v_hi[:, 4 * n:4 * n + 4, :].rearrange("p j d -> p (j d)").bitcast(F32),
                                             ALU.subtract).then_inc(v_lo_s, 1)

                    for what, n, h in WALK:
                        if what == "C":
                            chunk(n)
                            if n == 3:
                                v_low()
                            if n == 0:
                                dve.wait_ge(add_done, this(add_done, t, 0))
                                ln_front(1, b, g, 0)
                            if n == 3:
                                ln_normalise(1, b, g, 0)
                        if what == "S":
                            s = NT - 1 - n
                            nb, w = halves(n)
                            dve.wait_ge(s_done, this(s_done, t, QPG * s + h + 1))
                            at = (nb - 1) * CH + w - P
                            diagonal = score_banks(n, h)[:, at:at + P]
                            v_.tensor_tensor(diagonal, diagonal, mask_f[:, :], ALU.add).then_inc(masked, 1)
                            dve.wait_ge(masked, this(masked, t, QPG * s + h + 1))
                            v_.tensor_reduce(nmax[:, s % 2, h:h + 1],
                                             score_banks(n, h).rearrange("p (a n) -> p a n", a=nb)[:, :, 0:w],
                                             AX.XY, ALU.max, negate=True).then_inc(max_done, 1)
                        if what == "T":
                            dve.wait_ge(pth_done, this(pth_done, t, n + 1))
                            v_.tensor_tensor(pt_lo[:, n % 3, :], T[n % 2], pt_hi[:, n % 3, :].bitcast(F32),
                                             ALU.subtract).then_inc(ptl_done, 1)
                        if what == "V" and n == LAST[UNITS[n][0]]:
                            s = NT - 1 - UNITS[n][0]
                            dve.wait_ge(oh_done, this(oh_done, t, s + 1))
                            v_.tensor_tensor(o_lo[:, s % 2, :], O[s], o_hi[:, s % 2, :].bitcast(F32),
                                             ALU.subtract).then_inc(ol_done, 1)
                        if what == "Y":
                            s = NT - 1 - n
                            dve.wait_ge(y_done, this(y_done, t, s + 1))
                            row = x[:, bass.ds(b * NT + n, 1), :].rearrange("p a n -> p (a n)")
                            v_.tensor_tensor(row, O[s][:, 0:HID], row, ALU.add).then_inc(add_done, 1)

            def raw_low(n):
                if n == 1:
                    dve.wait_ge(rhi1_s, 1)
                else:
                    dve.wait_ge(rhi_s, n)
                v_.tensor_tensor(raw_lo[n % 2], raw[PIECES[n]], raw_hi[n % 2].bitcast(F32), ALU.subtract).then_inc(rlo_s, 1)

            def weights_low(n):
                piece = PIECES[n]
                for k in range(KH):
                    dve.wait_ge(fhi_s, n * KH + k + 1)
                    if piece < 4:
                        at = slice(piece * CH, (piece + 1) * CH)
                        v_.scalar_tensor_tensor(wu_lo[:, k, at], W[n][k], su_u[:, k:k + 1], wu_hi[:, k, at].bitcast(F32),
                                                ALU.mult, ALU.subtract).then_inc(wf_ok, 1)
                    else:
                        for one in range(2):
                            m = 2 * (piece - 4) + one
                            last = v_.scalar_tensor_tensor(wd_lo[k][:, m, :], W[n][k][:, one * HID:(one + 1) * HID],
                                                           su_d[:, 4 * k + m:4 * k + m + 1], wd_hi[k][:, m, :].bitcast(F32),
                                                           ALU.mult, ALU.subtract)
                        last.then_inc(wf_ok, 1)

            raw_low(1)

            def gated(c, m):
                dve.wait_ge(silu_s, c * NM + m + 1)
                v_.scalar_tensor_tensor(g32[:, m % 2, :], S[m % 2][:, CH:2 * CH], ws_u[:, m:m + 1], silu[:, m % 2, :],
                                        ALU.mult, ALU.mult).then_inc(g32_s, 1)
                dve.wait_ge(g32_s, c * NM + m + 3)
                v_.tensor_copy(g_hi[:, m % 2, :], g32[:, m % 2, :]).then_inc(ghi_s, 1)
                dve.wait_ge(ghi_s, c * NM + m + 1)
                v_.tensor_tensor(g_lo[:, m % 2, :], g32[:, m % 2, :], g_hi[:, m % 2, :].bitcast(F32),
                                 ALU.subtract).then_inc(g_ok, 1)

            def finish(c):
                dve.wait_ge(out_s, (c + 1) * 16)
                for a in range(2):
                    dve.wait_ge(ytr_s, (c + 1) * KH + a + 1)
                    v_.tensor_tensor(o_out[:, 2 * a:2 * a + 2, :], T[a].rearrange("p (j n) -> p j n", j=2),
                                     x[:, bass.ds(c * CT + 2 * a, 2), :], ALU.add).then_inc(fin_s, 1)

            for what, n in FIRST:
                if what == "P":
                    weights_low(n)
                    if 0 < n < len(PIECES) - 1:
                        raw_low(n + 1)
                    if n == 4:
                        ln_front(2, 0, 0, 0)
                        ln_normalise(2, 0, 0, 0)
                        ln_front(2, 0, 1, 0)
                if what == "G":
                    gated(0, n)
                if what == "L":
                    if n + 1 < NP:
                        ln_normalise(2, 0, n + 1, 0)
                    ln_high(2, 0, n, 0)
                    if n + 2 < NP:
                        ln_front(2, 0, n + 2, 0)
            with dve.Fori(1, B * NC_B) as c:
                gated(c, 0)
                gated(c, 1)
                finish(c - 1)
                for m in range(2, NM):
                    gated(c, m)
            finish(B * NC_B - 1)

        @block.tensor
        def _(pe):
            mm, tr = nc.tensor.matmul, nc.tensor.transpose
            for s, n in PER_PE.items():
                pe.sem_inc(s, n)
            pe.sem_inc(ytr_s, KH)

            def three(dst, w_h, w_l, r_h, r_l, start, stop):
                mm(dst, w_h, r_h, start=start, stop=False)
                mm(dst, w_h, r_l, start=False, stop=False)
                return mm(dst, w_l, r_h, start=False, stop=stop)

            for r, slots in enumerate(LN_SLOTS):
                pe.sem_inc(ln[r]["tr"], slots)

            def modulation(dst, v):
                for k in range(KH):
                    for a in range(KH):
                        last = mm(dst[:, k * B:(k + 1) * B], wmod_sb[:, a, v * HID + k * P:v * HID + (k + 1) * P],
                                  sc[:, 1, a, :], start=a == 0, stop=a == KH - 1)
                return last

            def ln_transpose(r, b, g, slot):
                n = ln_step(r, b, g, slot)[0]
                if r == 0:
                    pe.wait_ge(ln[r]["h32"], n + 1)
                elif r == 2 and n > 0:
                    pe.wait_ge(ln[r]["h32"], n)
                pe.wait_ge(ln[r]["xhat"], n + 1)
                for k in range(KH):
                    for j in range(LP):
                        last = tr(ln_bank(r, g, slot)[:, (k * LP + j) * P:(k * LP + j + 1) * P],
                                  xhat[slot][:, j, k * P:(k + 1) * P], ident[:, :])
                last.then_inc(ln[r]["tr"], 1)

            pe.wait_ge(silu_c, 1)
            pe.wait_ge(wmod_s[0], 16)
            for v in (SA, CA):
                last = modulation(S[0][:, v * KH * B:(v + 1) * KH * B], v)
            last.then_inc(mod_mm, 1)
            pe.wait_ge(ident_s, 16)
            for slot in range(2):
                ln_transpose(0, 0, 0, slot)
            pe.wait_ge(wmod_s[1], 16)
            for v in (SB, CB, GB):
                modulation(X[1][:, v * KH * B:(v + 1) * KH * B], v)
            for slot in range(2):
                ln_transpose(0, 0, 1, slot)
            for b in range(B):
                for a in range(KH):
                    last = mm(X[0][:, b * HID:(b + 1) * HID], scb[:, a, b, :], wmod_sb[:, a, GA * HID:(GA + 1) * HID],
                              start=a == 0, stop=a == KH - 1)
            last.then_inc(mod_mm, 1)
            pe.wait_ge(ln[0]["lo"], NP + LN_SLOTS[0])
            with pe.Fori(0, B) as b:
                with pe.Fori(0, NKV) as g:
                    t = b * NKV + g

                    def chunk(c):
                        what, h, half = CHUNKS[c]
                        if c == 0:
                            pe.wait_ge(exp_done, this(exp_done, t, 0))
                            pe.wait_ge(w_ready, t + 1)
                            pe.wait_ge(ln[1]["lo"], t + 1)
                        elif c == 3:
                            pe.wait_ge(add_done, this(add_done, t, 0))
                        elif c == 4:
                            pe.wait_ge(consts, 1)
                        elif c >= 6:
                            pe.wait_ge(qkv_lo, this(qkv_lo, t, c - 3))
                        at = {"q": h, "k": QPG, "v": QPG + 1}[what] * D
                        span = bass.ds(b * SEQ + half * CH, CH)
                        for k in range(KH):
                            last = three(bank(c), w_hi[:, k, at:at + D], w_lo[:, k, at:at + D],
                                         h_hi[:, k, span], h_lo[:, k, span], k == 0, k == KH - 1)
                        last.then_inc(qkv_done, 1)

                    def v_transpose():
                        pe.wait_ge(ptl_done, this(ptl_done, t, 0))
                        for n in range(2):
                            pe.wait_ge(vt_done, this(vt_done, t, n + 1))
                            for j in range(4):
                                last = tr(T[n][:, j * P:(j + 1) * P], vt[:, (4 * n + j) * P:(4 * n + j + 1) * P], ident[:, :])
                            last.then_inc(vtr_done, 1)

                    for what, n, h in WALK:
                        if what == "C":
                            chunk(n)
                        if what == "VT":
                            v_transpose()
                        if what == "L":
                            pe.wait_ge(v_lo_s, this(v_lo_s, t, 1))
                            ln_transpose(1, b, g, 0)
                        if what == "S":
                            s = NT - 1 - n
                            e = QPG * s + h
                            if e < QPG:
                                pe.wait_ge(qkv_lo, this(qkv_lo, t, 3 + e))
                            if e >= 2:
                                pe.wait_ge(exp_done, this(exp_done, t, e - 1 if n >= CT or n == CT - 1 and h < 2 else e - 3))
                            nb, w = halves(n)
                            wide = max(w, 2 * P)
                            q_at = slice(n * P, (n + 1) * P)
                            dst = score_banks(n, h)
                            for a in range(nb):
                                mm(dst[:, a * CH:a * CH + wide], q_hi[:, h, q_at], k_hi[:, a * w:a * w + wide],
                                   start=True, stop=False)
                            for a in range(nb):
                                mm(dst[:, a * CH:a * CH + wide], q_hi[:, h, q_at], k_lo[:, a * w:a * w + wide],
                                   start=False, stop=False)
                            for a in range(nb):
                                last = mm(dst[:, a * CH:a * CH + wide], q_lo[:, h, q_at], k_hi[:, a * w:a * w + wide],
                                          start=False, stop=True)
                            last.then_inc(s_done, 1)
                        if what == "T":
                            i, j = UNITS[n]
                            s = NT - 1 - i
                            if n >= 2:
                                pe.wait_ge(ptl_done, this(ptl_done, t, n - 1))
                            elif n == 1:
                                pe.wait_ge(v_lo_s, this(v_lo_s, t, 2))
                            else:
                                pe.wait_ge(ln[1]["hi"], t + 2)
                            for h in range(QPG):
                                if j == 0:
                                    pe.wait_ge(prob_done, this(prob_done, t, QPG * s + h + 1))
                                last = tr(T[n % 2][:, h * P:(h + 1) * P], prob[:, s % 2, h, j * P:(j + 1) * P], ident[:, :])
                            last.then_inc(t_done, 1)
                        if what == "V":
                            i, j = UNITS[n]
                            s = NT - 1 - i
                            if j == 0 and s == 0:
                                pe.wait_ge(qkv_lo, this(qkv_lo, t, 9))
                            elif j == 0 and s == 1:
                                pe.wait_ge(qkv_lo, this(qkv_lo, t, 10))
                            elif j == 0 and s < NT - 1:
                                pe.wait_ge(add_done, this(add_done, t, s - 1))
                            if n == 0:
                                pe.wait_ge(v_lo_s, this(v_lo_s, t, 2))
                            pe.wait_ge(ptl_done, this(ptl_done, t, n + 1))
                            three(O[s], v_hi[:, j, :], v_lo[:, j, :], pt_hi[:, n % 3, :], pt_lo[:, n % 3, :],
                                  j == 0, j == i).then_inc(pv_done, 1)
                        if what == "Y":
                            s = NT - 1 - n
                            if s == 0:
                                pe.wait_ge(wp_ready, t + 2)
                            pe.wait_ge(ol_done, this(ol_done, t, s + 1))
                            for h in range(QPG):
                                last = three(O[s][:, 0:HID], o_hi[:, s % 2, h * P:(h + 1) * P], o_lo[:, s % 2, h * P:(h + 1) * P],
                                             wp_hi[:, h, :], wp_lo[:, h, :], h == 0, h == QPG - 1)
                            last.then_inc(y_done, 1)

            def weights(n):
                if n == 0:
                    pe.wait_ge(ptl_done, (TURNS + 1) * NU)
                    pe.wait_ge(rlo0_s, 1)
                else:
                    if n > 1:
                        pe.wait_ge(wf_ok, KH * n)
                    pe.wait_ge(rlo_s, n)
                mats = had_r[PIECES[n] // 4]
                plus, minus = mats[:, 0:P], mats[:, P:2 * P]
                for k in range(KH):
                    for src in (0, 1):
                        mat = minus if k and src else plus
                        mm(W[n][k], mat, raw_hi[n % 2][:, src, :], start=not src, stop=False)
                        last = mm(W[n][k], mat, raw_lo[n % 2][:, src, :], start=False, stop=bool(src))
                    last.then_inc(fmm_s, 1)

            def gate_up(c, m):
                pe.wait_ge(g32_s, c * NM + m + 1)
                at = m // 2 * CH + m % 2 * P
                for a in (0, 1):
                    for k in range(KH):
                        col = at + (0 if a else 2 * P)
                        last = three(S[m % 2][:, a * CH:(a + 1) * CH], wu_hi[:, k, col:col + P], wu_lo[:, k, col:col + P],
                                     h_hi[:, k, bass.ds(c * CH, CH)], h_lo[:, k, bass.ds(c * CH, CH)],
                                     k == 0, k == KH - 1)
                last.then_inc(gu_s, 1)

            def down(c, m):
                if m == 0:
                    pe.wait_ge(yt_s, (c + 1) * KH)
                pe.wait_ge(g_ok, c * NM + m + 1)
                for k in range(KH):
                    last = three(X[k], wd_hi[m // 4][:, m % 4, k * P:(k + 1) * P], wd_lo[m // 4][:, m % 4, k * P:(k + 1) * P],
                                 g_hi[:, m % 2, :], g_lo[:, m % 2, :], m == 0, m == NM - 1)
                    if m == NM - 1:
                        last.then_inc(dn_s, 1)

            def back(c):
                pe.wait_ge(yt_s, (c + 2) * KH)
                for a in range(2):
                    pe.wait_ge(fin_s, c * 2 + a + 1)
                    for j in range(2):
                        for k in range(KH):
                            last = tr(T[a][:, j * HID + k * P:j * HID + (k + 1) * P],
                                      yt[:, k, (2 * a + j) * P:(2 * a + j + 1) * P], ident[:, :])
                    last.then_inc(ytr_s, 1)

            for what, n in FIRST:
                if what == "P":
                    weights(n)
                if what == "G":
                    if n == 0:
                        pe.wait_ge(ln[1]["lo"], TURNS + LN_SLOTS[1])
                    if n % 2 == 0:
                        pe.wait_ge(wf_ok, KH * (PIECES.index(n // 2) + 1))
                    gate_up(0, n)
                if what == "D":
                    if n in (0, 2):
                        pe.wait_ge(wf_ok, KH * (PIECES.index(4 + n // 2) + 1))
                    down(0, n)
                if what == "L":
                    if n == 0:
                        pe.wait_ge(wf_ok, KH * len(PIECES))
                    ln_transpose(2, 0, n, 0)
            with pe.Fori(1, B * NC_B) as c:
                gate_up(c, 0)
                down(c - 1, NM - 1)
                gate_up(c, 1)
                down(c, 0)
                back(c - 1)
                for m in range(2, NM):
                    gate_up(c, m)
                    down(c, m - 1)
                pe.wait_ge(ln[2]["lo"], NP + LN_SLOTS[2])
            down(B * NC_B - 1, NM - 1)
            back(B * NC_B - 1)


def kernel(**inputs):
    import concourse.bacc as bacc
    from concourse.bass_utils import run_bass_kernel_spmd

    def get(name):
        return np.asarray(inputs[name])

    x = np.ascontiguousarray(get("L0_attn_x").reshape(B * NT, P, HID))
    w = get("L0_attn_weight_qkv").reshape(NKV, GW, KH, P).transpose(0, 3, 2, 1).reshape(NKV, P, KH * GW)
    w = np.concatenate([w, w[:1]])
    wp = get("L0_attn_weight_proj").reshape(HID, NKV, QPG, D).transpose(1, 3, 2, 0).reshape(NKV, P, QPG * HID)
    up_gate = np.stack([get("L0_ffn_W_up"), get("L0_ffn_W_gate")]).reshape(2, 4, 2 * P, KH, P)
    wug = up_gate.transpose(1, 4, 3, 0, 2).reshape(4, P, KH * CH)
    wdn = get("L0_ffn_W_down").reshape(HID, 2, 2, 2, P)
    wdn = wdn.transpose(4, 2, 1, 3, 0).reshape(P, NM * HID)
    n = np.arange(P)
    had = np.array([[1.0]])
    while len(had) < P:
        had = np.block([[had, had], [had, -had]])
    had = np.concatenate([s * had / n ** 0.5 for n in (HID, INTER) for s in (1, -1)], axis=1).astype(np.float32)
    arrays = {
        "x": x, "wqkv": w, "wproj": wp, "wmod": get("L0_wmod"),
        "c": get("L0_c").reshape(B, KH, P).transpose(2, 1, 0), "wug": wug, "wdn": wdn,
        "su_ug": get("L0_ffn_SU_ug").reshape(KH, P).T, "su_dp": get("L0_ffn_SU_dp").reshape(NM, P).T,
        "ws_ug": get("L0_ffn_Wscale_ug").reshape(2 * NM, P).T, "ws_dp": get("L0_ffn_Wscale_dp").reshape(KH, P).T,
        "ident": np.eye(P, dtype=np.float32),
        "mask": np.where(n[None, :] > n[:, None], MASKED, 0.0).astype(np.float32), "had": had,
    }
    nc = bacc.Bacc("TRN2", target_bir_lowering=False, num_devices=1)
    feed, args = {}, []
    for name, a in arrays.items():
        a = np.ascontiguousarray(a)
        feed[f"in_{name}"] = a
        args.append(nc.dram_tensor(f"in_{name}", a.shape, mybir.dt.from_np(a.dtype), kind="ExternalInput").ap())
    args.append(nc.dram_tensor("out_y", (B * NT, P, HID), F32, kind="ExternalOutput").ap())
    build(nc, *args)
    r = run_bass_kernel_spmd(nc, [feed], core_ids=[0])
    return r.results[0]["out_y"].reshape(B, SEQ, HID)
```
